# Optimizing a Trainium2 kernel written in Bass

```python
import numpy as np
import jax
import jax.numpy as jnp

def _softmax(x, axis=-1):
    return jax.nn.softmax(x, axis=axis)

def _gelu(x):
    return jax.nn.gelu(x, approximate=True)

def _silu(x):
    return jax.nn.silu(x)

def _sigmoid(x):
    return jax.nn.sigmoid(x)

def _layernorm(x, axis=-1, eps=1e-05):
    m = jnp.mean(x, axis=axis, keepdims=True)
    v = jnp.var(x, axis=axis, keepdims=True)
    return (x - m) / jnp.sqrt(v + eps)

def _scatter_add(tgt, idx, src, axis=0):
    return tgt.at[idx].add(src)

def _segment_sum(src, seg, n):
    return jax.ops.segment_sum(src, seg, n)
kernel_name = 'mk_cond_seq_d2_seqx_r4_46331e'

def setup_inputs(seed: int=0):
    np.random.seed(seed)
    _w = jnp.asarray

    def _rec_inputs():
        import jax
        import jax.numpy as jnp
        _rk = jax.random.key(seed)
        x = -0.000125 + 0.9999 * jax.random.normal(jax.random.fold_in(_rk, 1), (8, 256, 256), jnp.float32)
        _lenS = 256 - jax.random.randint(jax.random.fold_in(_rk, 7), (8,), 0, max(1, 256 // 4) + 1, jnp.int32)
        _lenS2 = 256 - jax.random.randint(jax.random.fold_in(_rk, 8), (8,), 0, max(1, 256 // 4) + 1, jnp.int32)
        condB_t = jax.random.uniform(jax.random.fold_in(_rk, 11), (8,), jnp.float32, 0.0, 0.983423)
        itok_B_34_63 = jax.random.randint(jax.random.fold_in(_rk, 13), (8,), 34, 64, jnp.int32)
        fside_Bx16xSxS_0 = -1.47943e-05 + 1.00017 * jax.random.normal(jax.random.fold_in(_rk, 14), (8, 16, 256, 256), jnp.float32)
        _validS = jnp.arange(256)[None, :] < _lenS[:, None]
        _validS2 = jnp.arange(256)[None, :] < _lenS2[:, None]
        _causal = jnp.tril(jnp.ones((256, 256), dtype=bool))
        mask_Bx1xSxS_bk0 = jnp.logical_not(jnp.broadcast_to(_validS[:, None, None, :], (8, 1, 256, 256)))
        return (x, condB_t, itok_B_34_63, fside_Bx16xSxS_0, mask_Bx1xSxS_bk0)
    x, condB_t, itok_B_34_63, fside_Bx16xSxS_0, mask_Bx1xSxS_bk0 = _rec_inputs()

    def _L0_cond_setup():
        import jax, jax.numpy as jnp
        import numpy as np
        import math
        B, S, D, E = (32, 256, 256, 128)

        def _layer_norm(x, gamma, beta, eps=1e-05):
            mean = jnp.mean(x, axis=(-2, -1), keepdims=True)
            var = jnp.mean(jnp.square(x - mean), axis=(-2, -1), keepdims=True)
            return (x - mean) * jax.lax.rsqrt(var + eps) * gamma + beta

        def _noise_encoding(t, channels):
            half = channels // 2
            freqs = jnp.exp(jnp.arange(half, dtype=jnp.float32) * (-math.log(10000.0) / (half - 1)))
            emb = 5000.0 * t[:, None] * freqs[None, :]
            return jnp.concatenate([jnp.sin(emb), jnp.cos(emb)], axis=1)
        key = jax.random.key(seed)
        ks = jax.random.split(key, 20)

        def lin(k, fan_in, shape):
            return jax.random.normal(k, shape, jnp.float32) / np.sqrt(fan_in)
        inp = {'x': jax.random.normal(ks[0], (B, S, D), jnp.float32), 't': jax.random.uniform(ks[1], (B,), jnp.float32), 'W1': lin(ks[2], E, (E, 4 * E)), 'b1': jnp.zeros((4 * E,), jnp.float32), 'W2': lin(ks[3], 4 * E, (4 * E, 4 * E)), 'b2': jnp.zeros((4 * E,), jnp.float32), 'Wsc': lin(ks[4], 4 * E, (4 * E, D)), 'bsc': jnp.zeros((D,), jnp.float32), 'Wsh': lin(ks[5], 4 * E, (4 * E, D)), 'bsh': jnp.zeros((D,), jnp.float32), 'gamma': jnp.ones((S, D), jnp.float32), 'beta': jnp.zeros((S, D), jnp.float32), 'W_in': lin(ks[6], D, (D, D)), 'b_in': jnp.zeros((D,), jnp.float32), 'W_out': lin(ks[7], D, (D, D)), 'b_out': jnp.zeros((D,), jnp.float32)}
        return inp
    _L0_cond_all = _L0_cond_setup()
    _L0_cond_in = {k: v for k, v in _L0_cond_all.items() if k in ('W1', 'b1', 'W2', 'b2', 'Wsc', 'bsc', 'Wsh', 'bsh', 'gamma', 'beta', 'W_in', 'b_in', 'W_out', 'b_out')}
    del _L0_cond_all

    def _L1_cond_setup():
        import jax, jax.numpy as jnp
        import numpy as np
        import math
        D_MODEL = 256
        N_HEAD = 16
        HEAD_DIM = D_MODEL // N_HEAD
        D_FF = 1024
        NUM_STEPS = 100.0
        RESCALE = 4000.0
        EPS = 1e-05

        def _sin_emb(t):
            half = D_MODEL // 2
            x = t.astype(jnp.float32) / NUM_STEPS * RESCALE
            freqs = jnp.exp(jnp.arange(half, dtype=jnp.float32) * (-math.log(10000.0) / (half - 1)))
            e = x[:, None] * freqs[None, :]
            return jnp.concatenate([jnp.sin(e), jnp.cos(e)], axis=-1)

        def _ln(x):
            m = jnp.mean(x, axis=-1, keepdims=True)
            v = jnp.var(x, axis=-1, keepdims=True)
            return (x - m) / jnp.sqrt(v + EPS)

        def _gelu2(x):
            return x * jax.nn.sigmoid(1.702 * x)
        key = jax.random.key(seed)
        ks = jax.random.split(key, 24)
        B, S, D, F = (4, 128, D_MODEL, D_FF)
        std = 0.02
        inp = {'src': jax.random.normal(ks[0], (B, S, D), dtype=jnp.float32), 'src_mask': jax.random.randint(ks[1], (B, 1, S, S), 0, 2).astype(bool), 'timestep': jax.random.randint(ks[2], (B,), 0, 100, dtype=jnp.int32), 'attention_bias': jax.random.normal(ks[3], (B, N_HEAD, S, S), dtype=jnp.float32), 'W_ada': jax.random.normal(ks[4], (D, 2 * D), dtype=jnp.float32) * std, 'b_ada': jnp.zeros((2 * D,), dtype=jnp.float32), 'Wq': jax.random.normal(ks[5], (D, D), dtype=jnp.float32) * std, 'bq': jnp.zeros((D,), dtype=jnp.float32), 'Wk': jax.random.normal(ks[6], (D, D), dtype=jnp.float32) * std, 'bk': jnp.zeros((D,), dtype=jnp.float32), 'Wv': jax.random.normal(ks[7], (D, D), dtype=jnp.float32) * std, 'bv': jnp.zeros((D,), dtype=jnp.float32), 'Wo': jax.random.normal(ks[8], (D, D), dtype=jnp.float32) * std, 'bo': jnp.zeros((D,), dtype=jnp.float32), 'W1': jax.random.normal(ks[9], (D, F), dtype=jnp.float32) * std, 'b1': jnp.zeros((F,), dtype=jnp.float32), 'W2': jax.random.normal(ks[10], (F, D), dtype=jnp.float32) * std, 'b2': jnp.zeros((D,), dtype=jnp.float32), 'g2': jnp.ones((D,), dtype=jnp.float32), 'beta2': jnp.zeros((D,), dtype=jnp.float32)}
        return inp
    _L1_cond_all = _L1_cond_setup()
    _L1_cond_in = {k: v for k, v in _L1_cond_all.items() if k in ('W_ada', 'b_ada', 'Wq', 'bq', 'Wk', 'bk', 'Wv', 'bv', 'Wo', 'bo', 'W1', 'b1', 'W2', 'b2', 'g2', 'beta2')}
    del _L1_cond_all
    return {'x': x, 'condB_t': condB_t, 'itok_B_34_63': itok_B_34_63, 'fside_Bx16xSxS_0': fside_Bx16xSxS_0, 'mask_Bx1xSxS_bk0': mask_Bx1xSxS_bk0, 'L0_cond_W1': _L0_cond_in['W1'], 'L0_cond_b1': _L0_cond_in['b1'], 'L0_cond_W2': _L0_cond_in['W2'], 'L0_cond_b2': _L0_cond_in['b2'], 'L0_cond_Wsc': _L0_cond_in['Wsc'], 'L0_cond_bsc': _L0_cond_in['bsc'], 'L0_cond_Wsh': _L0_cond_in['Wsh'], 'L0_cond_bsh': _L0_cond_in['bsh'], 'L0_cond_gamma': _L0_cond_in['gamma'], 'L0_cond_beta': _L0_cond_in['beta'], 'L0_cond_W_in': _L0_cond_in['W_in'], 'L0_cond_b_in': _L0_cond_in['b_in'], 'L0_cond_W_out': _L0_cond_in['W_out'], 'L0_cond_b_out': _L0_cond_in['b_out'], 'L1_cond_W_ada': _L1_cond_in['W_ada'], 'L1_cond_b_ada': _L1_cond_in['b_ada'], 'L1_cond_Wq': _L1_cond_in['Wq'], 'L1_cond_bq': _L1_cond_in['bq'], 'L1_cond_Wk': _L1_cond_in['Wk'], 'L1_cond_bk': _L1_cond_in['bk'], 'L1_cond_Wv': _L1_cond_in['Wv'], 'L1_cond_bv': _L1_cond_in['bv'], 'L1_cond_Wo': _L1_cond_in['Wo'], 'L1_cond_bo': _L1_cond_in['bo'], 'L1_cond_W1': _L1_cond_in['W1'], 'L1_cond_b1': _L1_cond_in['b1'], 'L1_cond_W2': _L1_cond_in['W2'], 'L1_cond_b2': _L1_cond_in['b2'], 'L1_cond_g2': _L1_cond_in['g2'], 'L1_cond_beta2': _L1_cond_in['beta2']}

def reference(x, condB_t, itok_B_34_63, fside_Bx16xSxS_0, mask_Bx1xSxS_bk0, L0_cond_W1, L0_cond_b1, L0_cond_W2, L0_cond_b2, L0_cond_Wsc, L0_cond_bsc, L0_cond_Wsh, L0_cond_bsh, L0_cond_gamma, L0_cond_beta, L0_cond_W_in, L0_cond_b_in, L0_cond_W_out, L0_cond_b_out, L1_cond_W_ada, L1_cond_b_ada, L1_cond_Wq, L1_cond_bq, L1_cond_Wk, L1_cond_bk, L1_cond_Wv, L1_cond_bv, L1_cond_Wo, L1_cond_bo, L1_cond_W1, L1_cond_b1, L1_cond_W2, L1_cond_b2, L1_cond_g2, L1_cond_beta2):
    import jax
    import jax.numpy as jnp

    def _L0_cond_ref(x, t, W1, b1, W2, b2, Wsc, bsc, Wsh, bsh, gamma, beta, W_in, b_in, W_out, b_out):
        import jax, jax.numpy as jnp
        import numpy as np
        import math
        B, S, D, E = (32, 256, 256, 128)

        def _layer_norm(x, gamma, beta, eps=1e-05):
            mean = jnp.mean(x, axis=(-2, -1), keepdims=True)
            var = jnp.mean(jnp.square(x - mean), axis=(-2, -1), keepdims=True)
            return (x - mean) * jax.lax.rsqrt(var + eps) * gamma + beta

        def _noise_encoding(t, channels):
            half = channels // 2
            freqs = jnp.exp(jnp.arange(half, dtype=jnp.float32) * (-math.log(10000.0) / (half - 1)))
            emb = 5000.0 * t[:, None] * freqs[None, :]
            return jnp.concatenate([jnp.sin(emb), jnp.cos(emb)], axis=1)
        h = _noise_encoding(t, E)
        h = jax.nn.silu(h @ W1 + b1)
        h = h @ W2 + b2
        scale = (h @ Wsc + bsc)[:, None, :]
        shift = (h @ Wsh + bsh)[:, None, :]
        out = jax.nn.silu(scale * _layer_norm(x, gamma, beta) + shift)
        out = out @ W_in + b_in
        out = jax.nn.silu(scale * _layer_norm(out, gamma, beta) + shift)
        out = out @ W_out + b_out
        return out + x

    def _L1_cond_ref(src, src_mask, timestep, attention_bias, W_ada, b_ada, Wq, bq, Wk, bk, Wv, bv, Wo, bo, W1, b1, W2, b2, g2, beta2):
        import jax, jax.numpy as jnp
        import numpy as np
        import math
        D_MODEL = 256
        N_HEAD = 16
        HEAD_DIM = D_MODEL // N_HEAD
        D_FF = 1024
        NUM_STEPS = 100.0
        RESCALE = 4000.0
        EPS = 1e-05

        def _sin_emb(t):
            half = D_MODEL // 2
            x = t.astype(jnp.float32) / NUM_STEPS * RESCALE
            freqs = jnp.exp(jnp.arange(half, dtype=jnp.float32) * (-math.log(10000.0) / (half - 1)))
            e = x[:, None] * freqs[None, :]
            return jnp.concatenate([jnp.sin(e), jnp.cos(e)], axis=-1)

        def _ln(x):
            m = jnp.mean(x, axis=-1, keepdims=True)
            v = jnp.var(x, axis=-1, keepdims=True)
            return (x - m) / jnp.sqrt(v + EPS)

        def _gelu2(x):
            return x * jax.nn.sigmoid(1.702 * x)
        B, S, D = src.shape
        emb = jax.nn.silu(_sin_emb(timestep)) @ W_ada + b_ada
        scale, shift = jnp.split(emb[:, None, :], 2, axis=-1)
        x = _ln(src) * (1.0 + scale) + shift
        q = (x @ Wq + bq).reshape(B, S, N_HEAD, HEAD_DIM).transpose(0, 2, 1, 3)
        k = (x @ Wk + bk).reshape(B, S, N_HEAD, HEAD_DIM).transpose(0, 2, 1, 3)
        v = (x @ Wv + bv).reshape(B, S, N_HEAD, HEAD_DIM).transpose(0, 2, 1, 3)
        scores = jnp.einsum('bhqd,bhkd->bhqk', q / math.sqrt(HEAD_DIM), k)
        scores = scores + attention_bias
        scores = jnp.where(src_mask, -jnp.inf, scores.astype(jnp.float32))
        probs = jax.nn.softmax(scores, axis=-1).astype(v.dtype)
        ctx = jnp.einsum('bhqk,bhkd->bhqd', probs, v)
        ctx = ctx.transpose(0, 2, 1, 3).reshape(B, S, D)
        x = x + (ctx @ Wo + bo)
        h = _ln(x) * g2 + beta2
        ff = _gelu2(h @ W1 + b1) @ W2 + b2
        return x + ff
    x = _L0_cond_ref(x, condB_t, L0_cond_W1, L0_cond_b1, L0_cond_W2, L0_cond_b2, L0_cond_Wsc, L0_cond_bsc, L0_cond_Wsh, L0_cond_bsh, L0_cond_gamma, L0_cond_beta, L0_cond_W_in, L0_cond_b_in, L0_cond_W_out, L0_cond_b_out)
    x = _L1_cond_ref(x, mask_Bx1xSxS_bk0, itok_B_34_63, fside_Bx16xSxS_0, L1_cond_W_ada, L1_cond_b_ada, L1_cond_Wq, L1_cond_bq, L1_cond_Wk, L1_cond_bk, L1_cond_Wv, L1_cond_bv, L1_cond_Wo, L1_cond_bo, L1_cond_W1, L1_cond_b1, L1_cond_W2, L1_cond_b2, L1_cond_g2, L1_cond_beta2)
    return x

_drawn_inputs = setup_inputs


def setup_inputs(seed=0):
    import zlib

    import numpy as np

    out = dict(_drawn_inputs(seed))
    spreads = {'L0_cond_b1': (0.0, 0.1),
     'L0_cond_b2': (0.0, 0.1),
     'L0_cond_bsc': (0.0, 0.1),
     'L0_cond_bsh': (0.0, 0.1),
     'L0_cond_gamma': (1.0, 0.2),
     'L0_cond_beta': (0.0, 0.292),
     'L0_cond_b_in': (0.0, 0.1),
     'L0_cond_b_out': (0.0, 0.1),
     'L1_cond_b_ada': (0.0, 0.1),
     'L1_cond_bq': (0.0, 0.8),
     'L1_cond_bk': (0.0, 0.8),
     'L1_cond_bv': (0.0, 0.1),
     'L1_cond_bo': (0.0, 0.1),
     'L1_cond_b1': (0.0, 0.1),
     'L1_cond_b2': (0.0, 0.1),
     'L1_cond_g2': (1.0, 0.6),
     'L1_cond_beta2': (0.0, 0.68)}
    factors = {'fside_Bx16xSxS_0': 6.834, 'L1_cond_Wq': 8.0, 'L1_cond_Wk': 8.0}
    for name, (base, spread) in spreads.items():
        noise = np.random.default_rng([zlib.crc32(name.encode()), seed]).standard_normal(out[name].shape)
        drawn = base * np.exp(spread * noise) if base else spread * noise
        out[name] = jnp.asarray(drawn.astype(out[name].dtype))
    for name, factor in factors.items():
        out[name] = (out[name] * factor).astype(out[name].dtype)
    return out
```

```python
from contextlib import ExitStack

import concourse.bass as bass
from concourse import mybir

F32 = mybir.dt.float32
I32 = mybir.dt.int32
U8 = mybir.dt.uint8
ALU = mybir.AluOpType
ACT = mybir.ActivationFunctionType

P = 128
B, S, D = 8, 256, 256
H, DH = 16, 16
E = 128
HID = 4 * E
FF = 1024
NC = D // P
NF = FF // P
NH = HID // P
GROUPS, GH = 4, 4
EPS = 1e-5
MASKED = -1e30
HUGE = 3e38
MAGIC = 1.5 * 2 ** 23
TURN = 6.283185307179586
TURN1 = 6.28125
TURN2 = 2029 / 2 ** 20
TURN3 = TURN - TURN1 - TURN2
ARC = 3.1415925
SEED = 1597463007.0

COLS = {}
for _name, _n in (("b1", NH), ("b2", NH), ("bsc", NC), ("bsh", NC), ("b_in", NC), ("ada", 2 * NC),
                  ("bq", NC), ("bk", NC), ("ff1", NF), ("g2", NC), ("beta2", NC)):
    COLS[_name] = (sum(n for _, n in COLS.values()), _n)
NCOL = sum(n for _, n in COLS.values())
C_F0, C_T0, C_O0, C_F1, C_EVEN, C_ODD, NCST = range(7)
WAT = {}
for _name, _k, _n in (("in", NC, D), ("out", NC, D), ("q", NC, D), ("k", NC, D), ("v", NC, D),
                      ("o", NC, D), ("ff1", NC, FF), ("ff2", NF, D)):
    WAT[_name] = (sum(k * n for _, k, n in WAT.values()), _k, _n)
NW = sum(k * n for _, k, n in WAT.values())
CAT = {}
for _name, _k, _n in (("w1", 1, HID), ("w2", NH, HID), ("wsc", NH, D), ("wsh", NH, D), ("wada", NC, 2 * D)):
    CAT[_name] = (sum(k * n for _, k, n in CAT.values()), _k, _n)
NCW = sum(k * n for _, k, n in CAT.values())
R_OUT, R_V, R_O, R_FF2 = range(4)


def head_at(n):
    g, band = divmod(n, GH)
    chunk, odd = divmod(g, 2)
    return 8 * chunk + 2 * band + odd, band, chunk, odd


def hold(engine):
    engine.nop(nofuse=True)


class Chain:

    def __init__(self, sem, per, held=False):
        self.sem, self.per, self.held = sem, per, held

    def start(self, b, at=0):
        self.b, self.at = b, at
        return self

    def link(self, engine, instruction):
        self.at += 1
        assert self.at <= self.per
        instruction.then_inc(self.sem, 1)
        engine.wait_ge(self.sem, self.b * self.per + self.at)
        if self.held:
            hold(engine)


def need(engine, sem, value):
    if not isinstance(value, int) or value > 0:
        engine.wait_ge(sem, value)


def build(nc, x_tok, x_feat, cond_t, step_t, fside, mask, gbT, wmain, wcond, vecs, consts, rows, out):
    with ExitStack() as ctx:
        def sb(name, shape, dt=F32):
            return ctx.enter_context(nc.sbuf_tensor(name, shape, dt))

        def psum(name):
            return ctx.enter_context(nc.psum_tensor(name, [P, 512], F32))

        def sem(name):
            return ctx.enter_context(nc.semaphore(name))

        w = sb("w", [P, NW])
        cw = sb("cw", [P, NCW])
        gb = sb("gb", [P, 2, NC * S])
        vec = sb("vec", [P, NCOL])
        cst = sb("cst", [P, NCST])
        brow = sb("brow", [P, 4, D])
        ident = sb("ident", [P, P])
        mean_of = sb("mean_of", [P, P])
        tb = sb("tb", [P, B])
        tsi = sb("tsi", [P, B], I32)
        bns = sb("bns", [P, B, 6])
        bna = sb("bna", [P, B, 2])
        st1 = sb("st1", [P, 2, B])
        mean1 = sb("mean1", [P, B])
        rstd1 = sb("rstd1", [P, B])
        var1 = sb("var1", [P, B])
        angle = sb("angle", [P, 3, B])
        turns = sb("turns", [P, 3, B])
        emb = sb("emb", [P, 3, B])
        embh = sb("embh", [P, 3, B])
        h1 = sb("h1", [P, NH, B])
        h1t = sb("h1t", [P, NH, B])
        h2 = sb("h2", [P, NH, B])
        half_sc = sb("half_sc", [P, NC, B])
        half_sh = sb("half_sh", [P, NC, B])
        ada = sb("ada", [P, 2 * NC, B])
        bq4 = sb("bq4", [P, NC])
        bkp = sb("bkp", [P, 2, NC])

        xt = sb("xt", [P, NC * D])
        xf = sb("xf", [P, NC * S])
        xb = sb("xb", [P, NC * D])
        lna = sb("lna", [P, NC * S])
        lnz = sb("lnz", [P, NC * S])
        lny = sb("lny", [P, NC * S])
        lnt = sb("lnt", [P, NC * S])
        hin = sb("hin", [P, NC * S])
        mid = sb("mid", [P, NC * S])
        mst = sb("mst", [P, 6])
        mag = sb("mag", [P, 2])
        mst2 = sb("mst2", [P, 2])
        x1 = sb("x1", [P, NC, D])
        xn = sb("xn", [P, NC * D])
        xaT = sb("xaT", [P, NC, S])
        xres = sb("xres", [P, NC, S])
        qT = sb("qT", [P, NC, S])
        kT = sb("kT", [P, 2, NC, S])
        vpad = sb("vpad", [P, NC, H, 2 * DH])
        m8 = sb("m8", [P, NC * S], U8)
        maskneg = sb("maskneg", [P, NC * S])
        bias = sb("bias", [P, GROUPS, GH, NC * S])
        sneg = sb("sneg", [P, 2, NC, S])
        negmax = sb("negmax", [P, NC, H])
        prob = sb("prob", [P, 2, NC, S])
        rsum = sb("rsum", [P, NC, H])
        rinv = sb("rinv", [P, NC, H])
        rinvx = sb("rinvx", [P, NC, H, DH])
        probT = sb("probT", [P, 2 * GH, NC * S])
        rbc = sb("rbc", [P, NC * S])
        ctxT = sb("ctxT", [P, NC, S])
        x2 = sb("x2", [P, NC, D])
        x2b = sb("x2b", [P, NC * D])
        x2n = sb("x2n", [P, NC * D])
        hT = sb("hT", [P, NC, S])
        room = sb("room", [P, B, NC * S])
        uT = room[:, 0:NF // 2, :].rearrange("p a (m n) -> p (a m) n", m=2)
        uth = room[:, NF // 2:NF, :].rearrange("p a (m n) -> p (a m) n", m=2)
        xall = room
        fT = sb("fT", [P, NF, S])
        outt = sb("outt", [P, NC * D])

        def newton_buffers(name, n):
            return {k: sb(f"{name}_{k}", [P, n], I32 if k in ("h", "s") else F32) for k in "vhsnar"} | {
                "bs": sb(f"{name}_bs", [P, NC, 6]), "ba": sb(f"{name}_ba", [P, NC, 2])}

        ln2, ln3, ln4 = (newton_buffers(f"ln{i}", n) for i, n in ((2, 1), (3, NC), (4, NC)))

        score = [psum("score0"), psum("score1")]
        trans = [psum("trans0"), psum("trans1")]
        context = psum("context")
        M0, M1, M2 = psum("M0"), psum("M1"), psum("M2")

        def W(name):
            at, k, n = WAT[name]
            return w[:, at:at + k * n].rearrange("p (k n) -> p k n", k=k)

        def CW(name):
            at, k, n = CAT[name]
            return cw[:, at:at + k * n].rearrange("p (k n) -> p k n", k=k)

        def col(name, i=0, n=1):
            return vec[:, COLS[name][0] + i:COLS[name][0] + i + n]

        def halves(t):
            return t[:, :].rearrange("p (c n) -> p c n", c=2)

        small_loaded, weights_loaded, cond_loaded, xall_loaded = map(
            sem, ("small_loaded", "weights_loaded", "cond_loaded", "xall_loaded"))
        x_loaded, mask_loaded = sem("x_loaded"), sem("mask_loaded")
        bias_loaded = [sem(f"bias_loaded{g}") for g in range(GROUPS)]
        out_stored = sem("out_stored")
        ident_ready, zeros_ready = sem("ident_ready"), sem("zeros_ready")
        st1_ready, st1_done, var1_ready, std1_ready, angle_ready, emb_ready, embt_ready, embs_ready = map(
            sem, ("st1_ready", "st1_done", "var1_ready", "std1_ready", "angle_ready", "emb_ready",
                  "embt_ready", "embs_ready"))
        w1_done, h1_ready, h1t_ready, h1s_ready, w2_done, h2_ready, wsc_done, wada_done, setup_ready = map(
            sem, ("w1_done", "h1_ready", "h1t_ready", "h1s_ready", "w2_done", "h2_ready", "wsc_done",
                  "wada_done", "setup_ready"))
        v_setup = Chain(sem("v_setup"), 64)
        bias_ready, qk_done, smax_done, exp_done, tr_done, pt_done = map(
            sem, ("bias_ready", "qk_done", "smax_done", "exp_done", "tr_done", "pt_done"))
        pv_done = sem("pv_done")
        xb_ready, y_ready, tanh_ready, hin_ready, win_done, mid_ready = map(
            sem, ("xb_ready", "y_ready", "tanh_ready", "hin_ready", "win_done", "mid_ready"))
        mst_ready, mst_done, seed2, rs2, wout_done, x1_ready = map(
            sem, ("mst_ready", "mst_done", "seed2", "rs2", "wout_done", "x1_ready"))
        seed3, rs3, xn_ready, nt_done, xaT_ready, xres_ready = map(
            sem, ("seed3", "rs3", "xn_ready", "nt_done", "xaT_ready", "xres_ready"))
        q_done, k_done, v_done, qk_ready, v_ready = map(
            sem, ("q_done", "k_done", "v_done", "qk_ready", "v_ready"))
        mask_ready, mask_read = sem("mask_ready"), sem("mask_read")
        rinv_ready, rinvx_ready, r_done, r_ready, ctx_ready, wo_done, x2_ready = map(
            sem, ("rinv_ready", "rinvx_ready", "r_done", "r_ready", "ctx_ready", "wo_done", "x2_ready"))
        seed4, rs4, x2b_ready, x2n_ready, n2t_done, hT_ready = map(
            sem, ("seed4", "rs4", "x2b_ready", "x2n_ready", "n2t_done", "hT_ready"))
        ff1_done, u_ready, uth_ready, f_ready, ff2_done, out_ready = map(
            sem, ("ff1_done", "u_ready", "uth_ready", "f_ready", "ff2_done", "out_ready"))
        v_apply, v_ln2a, v_ln2b, v_ln3, v_ln4 = (
            Chain(sem(n), k) for n, k in (("v_apply", 4), ("v_ln2a", 2), ("v_ln2b", 4), ("v_ln3", 4), ("v_ln4", 4)))
        p_rs2, p_rs3, p_rs4 = (Chain(sem(n), 6, True) for n in ("p_rs2", "p_rs3", "p_rs4"))

        def mm(pe, o, lhsT, rhs, start=True, stop=True):
            return nc.tensor.matmul(o, lhsT, rhs, start=start, stop=stop)

        block = ctx.enter_context(nc.Block())

        def turns_of_the_loop(engine, turn):
            turn(-1, False, True, False)
            turn(0, True, True, False)
            with engine.Fori(1, B - 1) as b:
                turn(b, True, True, True)
            turn(B - 1, True, False, True)
            turn(B, False, False, True)

        @block.sync
        def _(sp):
            sp.dma_start(vec[:, :], vecs).then_inc(small_loaded, 16)
            sp.dma_start(cst[:, :], consts).then_inc(small_loaded, 16)
            sp.dma_start(tb[:, :], cond_t.partition_broadcast(P)).then_inc(small_loaded, 16)
            sp.dma_start(tsi[:, :], step_t.partition_broadcast(P)).then_inc(small_loaded, 16)
            sp.dma_start(cw[:, :], wcond).then_inc(cond_loaded, 16)
            sp.dma_start(xall[:, :, :], x_feat.rearrange("b p n -> p b n")).then_inc(xall_loaded, 16)
            sp.dma_start(gb[:, :, :], gbT).then_inc(weights_loaded, 16)
            sp.dma_start(brow[:, :, :], rows.partition_broadcast(P)).then_inc(weights_loaded, 16)
            sp.dma_start(w[:, :], wmain).then_inc(weights_loaded, 16)

            def turn(b, att, pre, post):
                if pre:
                    need(sp, xb_ready, b + 1)
                    need(sp, v_apply.sem, 4 * b + 1)
                    sp.dma_start(xt[:, :], x_tok[b + 1, :, :]).then_inc(x_loaded, 16)
                    sp.dma_start(xf[:, :], x_feat[b + 1, :, :]).then_inc(x_loaded, 16)
                    need(sp, mask_ready, b + 1)
                    sp.dma_start(m8[:, :], mask[b + 1, :, :]).then_inc(mask_loaded, 16)
                for g in range(GROUPS):
                    if post and g == GROUPS - 1:
                        sp.wait_ge(out_ready, b)
                        sp.dma_start(out[b - 1, :, :], outt[:, :]).then_inc(out_stored, 16)
                    if pre:
                        need(sp, smax_done, 16 * b + GH * (g + 1))
                        sp.dma_start(bias[:, g, :, :], fside[b + 1, g, :, :]).then_inc(bias_loaded[g], 16)

            turns_of_the_loop(sp, turn)
            sp.wait_ge(out_stored, 16 * B)

        @block.gpsimd
        def _(pool):
            nc.gpsimd.memset(ident[:, :], 0.0).then_inc(zeros_ready, 1)
            nc.gpsimd.memset(mean_of[:, :], 1.0 / P).then_inc(ident_ready, 1)
            nc.gpsimd.memset(vpad[:, :, :, :], 0.0).then_inc(ident_ready, 1)
            pool.wait_ge(zeros_ready, 1)
            nc.gpsimd.affine_select(out=ident[:, :], in_=ident[:, :], compare_op=ALU.not_equal, fill=1.0,
                                    base=0, pattern=[[-1, P]], channel_multiplier=1).then_inc(ident_ready, 1)

            def rsqrt(b, chain, t, n, seeded, done):
                c = chain.start(b)
                pool.wait_ge(seeded, b + 1)
                hold(pool)
                c.link(pool, nc.gpsimd.tensor_scalar(t["n"][:, :], t["v"][:, :], -0.5, None, ALU.mult))
                r = t["s"][:, :].bitcast(F32)
                for i in range(3):
                    for j in range(n):
                        a = nc.gpsimd.tensor_scalar(t["a"][:, j:j + 1], r[:, j:j + 1], r[:, j:j + 1],
                                                    t["n"][:, j:j + 1], ALU.mult, ALU.mult)
                    c.link(pool, a)
                    for j in range(n):
                        a = nc.gpsimd.tensor_scalar(t["r"][:, j:j + 1], t["a"][:, j:j + 1], 1.5,
                                                    r[:, j:j + 1], ALU.add, ALU.mult)
                    if i < 2:
                        c.link(pool, a)
                    r = t["r"][:, :]
                a.then_inc(done, 1)

            def mask_group(b, g):
                pool.wait_ge(bias_loaded[g], 16 * b + 16)
                for i in range(GH):
                    nc.gpsimd.tensor_tensor(bias[:, g, i, :], bias[:, g, i, :], maskneg[:, :],
                                            ALU.add).then_inc(bias_ready, 1)

            pool.wait_ge(weights_loaded, 48)

            def turn(b, att, pre, post):
                if att:
                    mask_group(b, GROUPS - 1)
                if pre:
                    need(pool, x1_ready, b + 1)
                    pool.wait_ge(x_loaded, 32 * b + 64)
                    nc.gpsimd.tensor_tensor(halves(xb), halves(xt),
                                            brow[:, R_OUT, :].unsqueeze(1).to_broadcast([P, NC, D]),
                                            ALU.add).then_inc(xb_ready, 1)
                if post:
                    rsqrt(b - 1, p_rs4, ln4, NC, seed4, rs4)
                    pool.wait_ge(x2_ready, b)
                    need(pool, out_ready, b - 1)
                    nc.gpsimd.tensor_tensor(halves(x2b), x2[:, :, :],
                                            brow[:, R_FF2, :].unsqueeze(1).to_broadcast([P, NC, D]),
                                            ALU.add).then_inc(x2b_ready, 1)
                if pre:
                    rsqrt(b + 1, p_rs2, ln2, 1, seed2, rs2)
                    pool.wait_ge(mask_loaded, 16 * b + 32)
                    need(pool, bias_ready, 16 * (b + 1))
                    hold(pool)
                    nc.gpsimd.tensor_scalar(maskneg[:, :], m8[:, :], MASKED, None, ALU.mult).then_inc(mask_ready, 1)
                    pool.wait_ge(mask_ready, b + 2)
                    mask_group(b + 1, 0)
                    rsqrt(b + 1, p_rs3, ln3, NC, seed3, rs3)
                    mask_group(b + 1, 1)
                    mask_group(b + 1, 2)

            turns_of_the_loop(pool, turn)

        @block.tensor
        def _(pe):
            pe.wait_ge(ident_ready, 3)
            pe.wait_ge(st1_ready, 1)
            mm(pe, M1[:, 0:2 * B], mean_of[:, :], st1[:, :, :]).then_inc(st1_done, 1)
            pe.wait_ge(cond_loaded, 16)
            pe.wait_ge(emb_ready, 1)
            for m in range(NH):
                last = mm(pe, M0[:, m * B:(m + 1) * B], CW("w1")[:, 0, m * P:(m + 1) * P], emb[:, 0, :])
            last.then_inc(w1_done, 1)
            pe.wait_ge(embs_ready, 1)
            for m in range(2 * NC):
                for k in range(NC):
                    last = mm(pe, M2[:, m * B:(m + 1) * B], CW("wada")[:, k, m * P:(m + 1) * P],
                              embh[:, 1 + k, :], k == 0, k == NC - 1)
            last.then_inc(wada_done, 1)
            pe.wait_ge(h1s_ready, 1)
            pe.wait_ge(var1_ready, 1)
            for m in range(NH):
                for k in range(NH):
                    last = mm(pe, M1[:, m * B:(m + 1) * B], CW("w2")[:, k, m * P:(m + 1) * P], h1[:, k, :],
                              k == 0, k == NH - 1)
            last.then_inc(w2_done, 1)
            pe.wait_ge(h2_ready, 1)
            for j, name in enumerate(("wsc", "wsh")):
                for m in range(NC):
                    for k in range(NH):
                        at = (j * NC + m) * B
                        last = mm(pe, M0[:, at:at + B], CW(name)[:, k, m * P:(m + 1) * P], h2[:, k, :],
                                  k == 0, k == NH - 1)
            last.then_inc(wsc_done, 1)
            pe.wait_ge(setup_ready, 1)

            def scores(b, n):
                h, band, c, odd = head_at(n)
                rows_ = slice(32 * band, 32 * band + 32)
                pe.wait_ge(qk_ready, 6 * b + 6)
                if n < 2:
                    need(pe, smax_done, 16 * b + n - 1)
                else:
                    pe.wait_ge(smax_done, 16 * b + n - 1)
                for t in range(NC):
                    last = mm(pe, score[n % 2][:, t * S:(t + 1) * S], qT[rows_, c, t * P:(t + 1) * P],
                              kT[rows_, odd, c, :])
                last.then_inc(qk_done, 1)

            def turn_probs(b, n):
                pe.wait_ge(exp_done, 16 * b + n + 1)
                need(pe, pt_done, 16 * b + n - 1)
                for k in range(NC):
                    for t in range(NC):
                        last = nc.tensor.transpose(trans[n % 2][:, k * S + t * P:k * S + (t + 1) * P],
                                                   prob[:, n % 2, t, k * P:(k + 1) * P], ident[:, :])
                last.then_inc(tr_done, 1)

            def values(b, g):
                pe.wait_ge(pt_done, 16 * b + GH * (g + 1))
                pe.wait_ge(v_ready, b + 1)
                if g == 0:
                    need(pe, ctx_ready, b)
                for k in range(NC):
                    for i in range(GH):
                        h, band, c, odd = head_at(GH * g + i)
                        last = mm(pe, context[32 * band:32 * band + 32, c * S:(c + 1) * S], vpad[:, k, h, :],
                                  probT[:, (g % 2) * GH + i, k * S:(k + 1) * S],
                                  k == 0 and odd == 0, k == NC - 1 and odd == 1)
                last.then_inc(pv_done, 1)

            def features_out(bank, name, src):
                for m in range(NC):
                    for k in range(NC):
                        last = mm(pe, bank[:, m * S:(m + 1) * S], W(name)[:, k, m * P:(m + 1) * P], src[:, k, :],
                                  k == 0, k == NC - 1)
                return last

            def tokens_out(bank, name, src, add=None):
                for t in range(NC):
                    for k in range(NC):
                        last = mm(pe, bank[:, t * D:(t + 1) * D], src[:, k, t * P:(t + 1) * P], W(name)[:, k, :],
                                  k == 0, k == NC - 1)
                    if add is not None:
                        for c in range(NC):
                            last = nc.tensor.matmul(bank[:, t * D + c * P:t * D + (c + 1) * P],
                                                    add[:, c, t * P:(t + 1) * P], ident[:, :],
                                                    start=False, stop=True, is_transpose=True,
                                                    skip_group_check=True)
                return last

            def turned(bank, src):
                for c in range(NC):
                    for t in range(NC):
                        last = nc.tensor.transpose(bank[:, c * S + t * P:c * S + (t + 1) * P],
                                                   src[:, t * D + c * P:t * D + (c + 1) * P], ident[:, :])
                return last

            def ff1(b, j, bank):
                pe.wait_ge(hT_ready, 2 * b)
                for i in range(2):
                    m = 2 * j + i
                    for k in range(NC):
                        last = mm(pe, bank[:, i * S:(i + 1) * S], W("ff1")[:, k, m * P:(m + 1) * P], hT[:, k, :],
                                  k == 0, k == NC - 1)
                last.then_inc(ff1_done, 1)

            def ff2(b, t):
                for k in range(NF):
                    last = mm(pe, M1[:, t * D:(t + 1) * D], fT[:, k, t * P:(t + 1) * P], W("ff2")[:, k, :],
                              k == 0, k == NF - 1)
                return last

            def filler(b, s, pre, post, att):
                if s == 1 and att:
                    need(pe, out_ready, b - 1)
                    pe.wait_ge(xaT_ready, 2 * b + 2)
                    tokens_out(M1, "v", xaT).then_inc(v_done, 1)
                if s == 1 and post:
                    if att:
                        pe.wait_ge(qk_ready, 6 * b + 6)
                    else:
                        pe.wait_ge(u_ready, 8 * b - 8)
                    pe.wait_ge(rinvx_ready, b)
                    for c in range(NC):
                        for t in range(NC):
                            last = nc.tensor.transpose(
                                M2[:, c * S + t * P:c * S + (t + 1) * P],
                                rinvx[:, t, 8 * c:8 * c + 8, :].rearrange("p h d -> p (h d)"), ident[:, :])
                    last.then_inc(r_done, 1)
                if s == 3 and post:
                    pe.wait_ge(ctx_ready, b)
                    if att:
                        pe.wait_ge(v_ready, b + 1)
                    else:
                        pe.wait_ge(out_ready, b - 1)
                    pe.wait_ge(xres_ready, b)
                    tokens_out(M1, "o", ctxT, xres).then_inc(wo_done, 1)
                if s == 4 and pre:
                    pe.wait_ge(hin_ready, 2 * b + 3)
                    need(pe, qk_ready, 6 * b + 6)
                    features_out(M0, "in", halves(hin)).then_inc(win_done, 1)
                if s == 5 and post:
                    pe.wait_ge(x2n_ready, b)
                    pe.wait_ge(r_ready, b)
                    turned(M2, x2n).then_inc(n2t_done, 1)
                if s == 6 and pre:
                    pe.wait_ge(mst_ready, b + 2)
                    pe.wait_ge(mid_ready, 2 * b + 4)
                    mm(pe, M0[:, 0:2], mean_of[:, :], mag[:, :]).then_inc(mst_done, 1)
                if s in (6, 7, 8, 9) and post:
                    j = s - 6
                    if j == 0:
                        pe.wait_ge(x2_ready, b)
                    if j >= 2:
                        pe.wait_ge(u_ready, 8 * b - 8 + 2 * (j - 1))
                    ff1(b, j, (M1, M2)[j % 2])
                if s == 8 and pre:
                    pe.wait_ge(hin_ready, 2 * b + 4)
                    pe.wait_ge(v_ln2b.sem, 4 * b + 5)
                    tokens_out(M0, "out", halves(hin)).then_inc(wout_done, 1)
                if s == 11 and pre:
                    pe.wait_ge(xn_ready, b + 2)
                    turned(M0, xn).then_inc(nt_done, 1)
                if s == 11 and post:
                    pe.wait_ge(f_ready, 4 * b)
                    ff2(b, 0)
                if s == 12 and post:
                    ff2(b, 1).then_inc(ff2_done, 1)
                if s == 13 and pre:
                    pe.wait_ge(xaT_ready, 2 * b + 4)
                    features_out(M0, "q", xaT).then_inc(q_done, 1)
                if s == 14 and pre:
                    need(pe, u_ready, 8 * b)
                    features_out(M2, "k", xaT).then_inc(k_done, 1)

            def turn(b, att, pre, post):
                for s in range(16):
                    if att:
                        scores(b, s)
                    if s == 1 and post:
                        values(b - 1, GROUPS - 1)
                    if att and s % 4 == 1 and s > 1:
                        values(b, s // 4 - 1)
                    filler(b, s, pre, post, att)
                    if s == 0:
                        if post:
                            turn_probs(b - 1, 15)
                    elif att:
                        turn_probs(b, s - 1)

            turns_of_the_loop(pe, turn)

        @block.scalar
        def _(act):
            act.wait_ge(angle_ready, 1)
            nc.scalar.activation(emb[:, :, :], angle[:, :, :], ACT.Sin).then_inc(emb_ready, 1)
            act.wait_ge(emb_ready, 1)
            nc.scalar.activation(embh[:, :, :], emb[:, :, :], ACT.Tanh, scale=0.5).then_inc(embt_ready, 1)
            act.wait_ge(h1_ready, 1)
            nc.scalar.activation(h1t[:, :, :], h1[:, :, :], ACT.Tanh, scale=0.5).then_inc(h1t_ready, 1)
            act.wait_ge(var1_ready, 1)
            nc.scalar.activation(rstd1[:, :], var1[:, :], ACT.Sqrt).then_inc(std1_ready, 1)

            def exps(b, n):
                h = head_at(n)[0]
                act.wait_ge(smax_done, 16 * b + n + 1)
                need(act, tr_done, 16 * b + n - 1)
                if n == 0:
                    need(act, rinv_ready, b)
                for t in range(NC):
                    last = nc.scalar.activation(prob[:, n % 2, t, :], sneg[:, n % 2, t, :], ACT.Exp,
                                                bias=negmax[:, t, h:h + 1], scale=-1.0,
                                                accum_out=rsum[:, t, h:h + 1])
                last.then_inc(exp_done, 1)

            def tanh_of(b, k):
                act.wait_ge(y_ready, 2 * b + 3 + k)
                need(act, hin_ready, 2 * b + 2 + k)
                nc.scalar.activation(lnt[:, :], lny[:, :], ACT.Tanh).then_inc(tanh_ready, 1)

            def filler(b, s, pre, post, att):
                if s == 1 and post:
                    act.wait_ge(r_done, b)
                    need(act, ctx_ready, b - 1)
                    nc.scalar.activation(rbc[:, :], M2[:, :], ACT.Copy).then_inc(r_ready, 1)
                if s == 2 and pre:
                    tanh_of(b, 0)
                if s == 4 and pre:
                    act.wait_ge(win_done, b + 2)
                    for m in range(NC):
                        nc.scalar.activation(mid[:, m * S:(m + 1) * S], M0[:, m * S:(m + 1) * S], ACT.Identity,
                                             bias=col("b_in", m)).then_inc(mid_ready, 1)
                if s == 5 and post:
                    act.wait_ge(n2t_done, b)
                    for c in range(NC):
                        nc.scalar.activation(hT[:, c, :], M2[:, c * S:(c + 1) * S], ACT.Identity,
                                             bias=col("beta2", c), scale=col("g2", c)).then_inc(hT_ready, 1)
                if s in (6, 7, 8, 9) and post:
                    j = s - 6
                    act.wait_ge(ff1_done, 4 * b - 4 + j + 1)
                    bank = (M1, M2)[j % 2]
                    need(act, f_ready, 4 * (b - 1))
                    for i in range(2):
                        m = 2 * j + i
                        nc.scalar.activation(uT[:, m, :], bank[:, i * S:(i + 1) * S], ACT.Identity,
                                             bias=col("ff1", m)).then_inc(u_ready, 1)
                    act.wait_ge(u_ready, 8 * b - 8 + 2 * (j + 1))
                    nc.scalar.activation(uth[:, 2 * j:2 * j + 2, :], uT[:, 2 * j:2 * j + 2, :], ACT.Tanh,
                                         scale=0.5 * 1.702).then_inc(uth_ready, 1)
                if s == 7 and pre:
                    tanh_of(b, 1)
                if s == 11 and pre:
                    act.wait_ge(nt_done, b + 2)
                    if att:
                        act.wait_ge(v_done, b + 1)
                        act.wait_ge(xres_ready, b + 1)
                    for c in range(NC):
                        at = ada[:, NC + c, bass.ds(b + 1, 1)]
                        nc.scalar.activation(xaT[:, c, :], M0[:, c * S:(c + 1) * S], ACT.Identity,
                                             bias=at, scale=ada[:, c, bass.ds(b + 1, 1)]).then_inc(xaT_ready, 1)
                if s == 15 and pre:
                    need(act, qk_done, 16 * (b + 1))
                    act.wait_ge(q_done, b + 2)
                    for c in range(NC):
                        nc.scalar.activation(qT[:, c, :], M0[:, c * S:(c + 1) * S], ACT.Identity,
                                             bias=bq4[:, c:c + 1], scale=DH ** -0.5).then_inc(qk_ready, 1)
                    act.wait_ge(k_done, b + 2)
                    for c in range(NC):
                        for odd in range(2):
                            nc.scalar.activation(kT[:, odd, c, :], M2[:, c * S:(c + 1) * S], ACT.Identity,
                                                 bias=bkp[:, odd, c:c + 1],
                                                 scale=cst[:, C_EVEN + odd:C_EVEN + odd + 1]).then_inc(qk_ready, 1)

            def turn(b, att, pre, post):
                for s in range(16):
                    if s == 15:
                        filler(b, s, pre, post, att)
                    if att:
                        exps(b, s)
                    if s != 15:
                        filler(b, s, pre, post, att)

            act.wait_ge(setup_ready, 1)
            turns_of_the_loop(act, turn)

        @block.vector
        def _(dve):
            v = nc.vector
            c = v_setup.start(0)

            dve.wait_ge(xall_loaded, 16)
            for i in range(B):
                last = v.bn_stats(bns[:, i, :], xall[:, i, :])
            c.link(dve, last)
            for i in range(B):
                last = v.bn_aggr(bna[:, i, :], bns[:, i, :])
            c.link(dve, last)
            v.tensor_copy(st1[:, 0, :], bna[:, :, 0])
            c.link(dve, v.tensor_tensor(st1[:, 1, :], bna[:, :, 0], bna[:, :, 0], ALU.mult))
            v.tensor_tensor(st1[:, 1, :], st1[:, 1, :], bna[:, :, 1], ALU.add).then_inc(st1_ready, 1)

            dve.wait_ge(small_loaded, 64)
            v.tensor_scalar(tb[:, :], tb[:, :], 5000.0, None, ALU.mult)
            c.link(dve, v.tensor_copy(angle[:, 2, :], tsi[:, :]))
            c.link(dve, v.tensor_scalar(angle[:, 2, :], angle[:, 2, :], 0.01, 4000.0, ALU.mult, ALU.mult))
            v.tensor_scalar(angle[:, 0, :], tb[:, :], cst[:, C_F0:C_F0 + 1], None, ALU.mult)
            v.tensor_scalar(angle[:, 1, :], angle[:, 2, :], cst[:, C_F1:C_F1 + 1], None, ALU.mult)
            c.link(dve, v.tensor_scalar(angle[:, 2, :], angle[:, 2, :], cst[:, C_F1:C_F1 + 1], None, ALU.mult))
            v.tensor_scalar(turns[:, 0, :], angle[:, 0, :], 1 / TURN, cst[:, C_T0:C_T0 + 1], ALU.mult, ALU.add)
            v.tensor_scalar(turns[:, 1, :], angle[:, 1, :], 1 / TURN, None, ALU.mult)
            c.link(dve, v.tensor_scalar(turns[:, 2, :], angle[:, 2, :], 1 / TURN, 0.25, ALU.mult, ALU.add))
            c.link(dve, v.tensor_scalar(turns[:, :, :], turns[:, :, :], MAGIC, None, ALU.add))
            c.link(dve, v.tensor_scalar(turns[:, :, :], turns[:, :, :], MAGIC, None, ALU.subtract))
            for part in (TURN1, TURN2, TURN3):
                c.link(dve, v.scalar_tensor_tensor(out=angle[:, :, :], in0=turns[:, :, :], scalar=-part,
                                                   in1=angle[:, :, :], op0=ALU.mult, op1=ALU.add))
            v.tensor_scalar(angle[:, 0, :], angle[:, 0, :], cst[:, C_O0:C_O0 + 1], None, ALU.add)
            c.link(dve, v.tensor_scalar(angle[:, 2, :], angle[:, 2, :], TURN / 4, None, ALU.add))
            v.tensor_scalar(angle[:, :, :], angle[:, :, :], ARC, -ARC, ALU.min, ALU.max).then_inc(angle_ready, 1)

            def silu(t, x):
                c.link(dve, v.scalar_tensor_tensor(out=x, in0=t, scalar=1.0, in1=x, op0=ALU.add, op1=ALU.mult))
                return v.tensor_scalar(x, x, 0.5, None, ALU.mult)

            def plus_col(o, x, name, n):
                return v.tensor_tensor(o, x, col(name, 0, n).unsqueeze(2).to_broadcast([P, n, B]), ALU.add)

            def small(bank, at, n):
                return bank[:, at * B:(at + n) * B].rearrange("p (m b) -> p m b", b=B)

            dve.wait_ge(w1_done, 1)
            plus_col(h1[:, :, :], small(M0, 0, NH), "b1", NH).then_inc(h1_ready, 1)
            dve.wait_ge(embt_ready, 1)
            c.link(dve, v.scalar_tensor_tensor(out=embh[:, :, :], in0=embh[:, :, :], scalar=1.0,
                                               in1=emb[:, :, :], op0=ALU.add, op1=ALU.mult))
            v.tensor_scalar(embh[:, :, :], embh[:, :, :], 0.5, None, ALU.mult).then_inc(embs_ready, 1)
            dve.wait_ge(st1_done, 1)
            c.link(dve, v.tensor_copy(mean1[:, :], M1[:, 0:B]))
            c.link(dve, v.tensor_tensor(var1[:, :], mean1[:, :], mean1[:, :], ALU.mult))
            c.link(dve, v.scalar_tensor_tensor(out=var1[:, :], in0=var1[:, :], scalar=-1.0, in1=M1[:, B:2 * B],
                                               op0=ALU.mult, op1=ALU.add))
            v.tensor_scalar(var1[:, :], var1[:, :], EPS, None, ALU.add).then_inc(var1_ready, 1)
            dve.wait_ge(h1t_ready, 1)
            silu(h1t[:, :, :], h1[:, :, :]).then_inc(h1s_ready, 1)
            dve.wait_ge(wada_done, 1)
            c.link(dve, plus_col(ada[:, :, :], small(M2, 0, 2 * NC), "ada", 2 * NC))
            v.tensor_scalar(ada[:, 0:NC, :], ada[:, 0:NC, :], 1.0, None, ALU.add)
            v.tensor_scalar(bq4[:, :], col("bq", 0, NC), DH ** -0.5, None, ALU.mult)
            for odd in range(2):
                v.tensor_scalar(bkp[:, odd, :], col("bk", 0, NC), cst[:, C_EVEN + odd:C_EVEN + odd + 1], None, ALU.mult)
            dve.wait_ge(w2_done, 1)
            plus_col(h2[:, :, :], small(M1, 0, NH), "b2", NH).then_inc(h2_ready, 1)
            dve.wait_ge(std1_ready, 1)
            v.reciprocal(rstd1[:, :], rstd1[:, :])
            dve.wait_ge(weights_loaded, 48)
            v.tensor_scalar(W("ff2"), W("ff2"), 0.5, None, ALU.mult)
            dve.wait_ge(wsc_done, 1)
            plus_col(half_sc[:, :, :], small(M0, 0, NC), "bsc", NC)
            c.link(dve, plus_col(half_sh[:, :, :], small(M0, NC, NC), "bsh", NC))
            v.tensor_scalar(half_sc[:, :, :], half_sc[:, :, :], 0.5, None, ALU.mult)
            c.link(dve, v.tensor_scalar(half_sh[:, :, :], half_sh[:, :, :], 0.5, None, ALU.mult))
            c.link(dve, v.tensor_copy(st1[:, 0, :], half_sh[:, 0, :]))
            v.tensor_copy(st1[:, 0, :], half_sh[:, 0, :]).then_inc(setup_ready, 1)

            def softmax_max(b, n):
                h = head_at(n)[0]
                dve.wait_ge(qk_done, 16 * b + n + 1)
                dve.wait_ge(bias_ready, 16 * b + n + 1)
                need(dve, exp_done, 16 * b + n - 1)
                for t in range(NC):
                    if t == 0:
                        hold(dve)
                    last = v.tensor_tensor_reduce(
                        out=sneg[:, n % 2, t, :], in0=score[n % 2][:, t * S:(t + 1) * S],
                        in1=bias[:, n // GH, n % GH, t * S:(t + 1) * S], scale=-1.0, scalar=HUGE,
                        op0=ALU.add, op1=ALU.min, accum_out=negmax[:, t, h:h + 1])
                last.then_inc(smax_done, 1)

            def probs_out(b, n):
                dve.wait_ge(tr_done, 16 * b + n + 1)
                need(dve, pv_done, 4 * b + n // GH - 1)
                v.tensor_copy(probT[:, n % 8, :], trans[n % 2][:, :]).then_inc(pt_done, 1)

            def apply(b, k, src, mean, rstd):
                c = v_apply.start(b, 2 * k)
                c.link(dve, v.scalar_tensor_tensor(out=lna[:, :], in0=src, scalar=mean, in1=gb[:, 0, :],
                                                   op0=ALU.subtract, op1=ALU.mult))
                c.link(dve, v.scalar_tensor_tensor(out=lnz[:, :], in0=lna[:, :], scalar=rstd, in1=gb[:, 1, :],
                                                   op0=ALU.mult, op1=ALU.add))
                for m in range(NC):
                    last = v.tensor_scalar(lny[:, m * S:(m + 1) * S], lnz[:, m * S:(m + 1) * S],
                                           half_sc[:, m, bass.ds(b, 1)], half_sh[:, m, bass.ds(b, 1)],
                                           ALU.mult, ALU.add)
                last.then_inc(y_ready, 1)

            def silu_out(b, k):
                dve.wait_ge(tanh_ready, 2 * b + 1 + k)
                if k == 0:
                    need(dve, wout_done, b)
                else:
                    dve.wait_ge(win_done, b + 1)
                v.scalar_tensor_tensor(out=hin[:, :], in0=lnt[:, :], scalar=1.0, in1=lny[:, :],
                                       op0=ALU.add, op1=ALU.mult).then_inc(hin_ready, 1)

            def seed(b, c, t, seeded):
                c.link(dve, v.tensor_scalar(t["h"][:, :], t["v"][:, :].bitcast(I32), 1, None,
                                            ALU.arith_shift_right))
                v.tensor_scalar(t["s"][:, :], t["h"][:, :], -1.0, SEED, ALU.mult, ALU.add).then_inc(seeded, 1)

            def token_stats(b, chain, t, x, seeded):
                c = chain.start(b)
                for i in range(NC):
                    last = v.bn_stats(t["bs"][:, i, :], x[:, i, :])
                c.link(dve, last)
                hold(dve)
                for i in range(NC):
                    last = v.bn_aggr(t["ba"][:, i, :], t["bs"][:, i, :])
                c.link(dve, last)
                c.link(dve, v.tensor_scalar(t["v"][:, :], t["ba"][:, :, 1], EPS, None, ALU.add))
                seed(b, c, t, seeded)

            def token_norm(o, x, t):
                for i in range(NC):
                    last = v.tensor_scalar(o[:, i * D:(i + 1) * D], x[:, i, :], t["ba"][:, i, 0:1],
                                           t["r"][:, i:i + 1], ALU.subtract, ALU.mult)
                return last

            def before(b, s, pre, post, att):
                if s == 0 and post:
                    dve.wait_ge(exp_done, 16 * b)
                    v.reciprocal(rinv[:, :, :], rsum[:, :, :]).then_inc(rinv_ready, 1)
                    dve.wait_ge(rinv_ready, b)
                    need(dve, r_done, b - 1)
                    v.tensor_copy(rinvx[:, :, :, :], rinv[:, :, :].unsqueeze(3).to_broadcast([P, NC, H, DH]))\
                     .then_inc(rinvx_ready, 1)
                if s == 1 and pre:
                    dve.wait_ge(x_loaded, 32 * b + 64)
                    apply(b + 1, 0, xf[:, :], mean1[:, bass.ds(b + 1, 1)], rstd1[:, bass.ds(b + 1, 1)])
                if s == 2 and post:
                    dve.wait_ge(pv_done, 4 * b)
                    dve.wait_ge(r_ready, b)
                    v.tensor_tensor(ctxT[:, :, :], halves(context), halves(rbc), ALU.mult).then_inc(ctx_ready, 1)
                if s == 4 and post:
                    dve.wait_ge(wo_done, b)
                    need(dve, x2b_ready, b - 1)
                    v.tensor_tensor(x2[:, :, :], halves(M1), brow[:, R_O, :].unsqueeze(1).to_broadcast([P, NC, D]),
                                    ALU.add).then_inc(x2_ready, 1)
                    dve.wait_ge(x2_ready, b)
                    token_stats(b - 1, v_ln4, ln4, x2, seed4)
                if s == 4 and att:
                    dve.wait_ge(xaT_ready, 2 * b + 2)
                    v.tensor_copy(xres[:, :, :], xaT[:, :, :]).then_inc(xres_ready, 1)
                if s == 5 and post:
                    dve.wait_ge(rs4, b)
                    token_norm(x2n, x2, ln4).then_inc(x2n_ready, 1)
                if s == 7 and pre:
                    dve.wait_ge(rs2, b + 2)
                    apply(b + 1, 1, mid[:, :], mst2[:, 0:1], ln2["r"][:, 0:1])
                if s == 9 and pre:
                    dve.wait_ge(wout_done, b + 2)
                    dve.wait_ge(xb_ready, b + 2)
                    v.tensor_tensor(x1[:, :, :], halves(M0), halves(xb), ALU.add).then_inc(x1_ready, 1)
                    dve.wait_ge(x1_ready, b + 2)
                    token_stats(b + 1, v_ln3, ln3, x1, seed3)
                if s == 10 and pre:
                    dve.wait_ge(rs3, b + 2)
                    token_norm(xn, x1, ln3).then_inc(xn_ready, 1)
                if s == 13 and post:
                    dve.wait_ge(ff2_done, b)
                    dve.wait_ge(x2b_ready, b)
                    need(dve, out_stored, 16 * (b - 1))
                    v.tensor_tensor(outt[:, :], M1[:, :], x2b[:, :], ALU.add).then_inc(out_ready, 1)

            def after(b, s, pre, post, att):
                if s == 1 and att:
                    dve.wait_ge(v_done, b + 1)
                    need(dve, pv_done, 4 * b)
                    for odd in range(2):
                        src = M1[:, :].rearrange("p (t h o d) -> p t h o d", t=NC, o=2, d=DH)[:, :, :, odd, :]
                        dst = vpad[:, :, :, odd * DH:(odd + 1) * DH].rearrange("p t (h o) d -> p t h o d", o=2)
                        bv = brow[:, R_V, :].rearrange("p (h o d) -> p h o d", o=2, d=DH)[:, :, odd, :]
                        for t in range(NC):
                            last = v.tensor_tensor(dst[:, t, :, odd, :], src[:, t, :, :], bv, ALU.add)
                    last.then_inc(v_ready, 1)
                if s == 2 and pre:
                    silu_out(b + 1, 0)
                if s == 5 and pre:
                    c = v_ln2a.start(b + 1)
                    dve.wait_ge(mid_ready, 2 * b + 4)
                    c.link(dve, v.bn_stats(mst[:, :], mid[:, :]))
                    hold(dve)
                    c.link(dve, v.bn_aggr(ln2["ba"][:, 0, :], mst[:, :]))
                    v.tensor_copy(mag[:, 0:1], ln2["ba"][:, 0, 0:1])
                    v.scalar_tensor_tensor(out=mag[:, 1:2], in0=ln2["ba"][:, 0, 0:1], scalar=ln2["ba"][:, 0, 0:1],
                                           in1=ln2["ba"][:, 0, 1:2], op0=ALU.mult, op1=ALU.add)\
                     .then_inc(mst_ready, 1)
                if s == 6 and pre:
                    c = v_ln2b.start(b + 1)
                    dve.wait_ge(mst_done, b + 2)
                    c.link(dve, v.tensor_copy(mst2[:, :], M0[:, 0:2]))
                    c.link(dve, v.scalar_tensor_tensor(out=ln2["a"][:, :], in0=mst2[:, 0:1], scalar=mst2[:, 0:1],
                                                       in1=mst2[:, 1:2], op0=ALU.mult, op1=ALU.subtract))
                    c.link(dve, v.tensor_scalar(ln2["v"][:, :], ln2["a"][:, :], -1.0, EPS, ALU.mult, ALU.add))
                    seed(b + 1, c, ln2, seed2)
                if s == 7 and pre:
                    silu_out(b + 1, 1)
                if s in (7, 8, 9, 10) and post:
                    j = s - 7
                    dve.wait_ge(uth_ready, 4 * b - 4 + j + 1)
                    if j == 0:
                        need(dve, ff2_done, b - 1)
                    v.scalar_tensor_tensor(out=fT[:, 2 * j:2 * j + 2, :], in0=uth[:, 2 * j:2 * j + 2, :],
                                           scalar=1.0, in1=uT[:, 2 * j:2 * j + 2, :], op0=ALU.add,
                                           op1=ALU.mult).then_inc(f_ready, 1)

            def turn(b, att, pre, post):
                for s in range(16):
                    if att:
                        softmax_max(b, s)
                    before(b, s, pre, post, att)
                    if s == 0:
                        if post:
                            probs_out(b - 1, 15)
                    elif att:
                        probs_out(b, s - 1)
                    after(b, s, pre, post, att)

            turns_of_the_loop(dve, turn)


def kernel(**inputs):
    import numpy as np
    import concourse.bacc as bacc
    from concourse.bass_utils import run_bass_kernel_spmd as run

    a = {k: np.asarray(x) for k, x in inputs.items()}

    def columns(x):
        return x.reshape(-1, P).T

    def rows_of(x):
        return x.reshape(-1, P, x.shape[1]).transpose(1, 0, 2).reshape(P, -1)

    half0, half1 = E // 2, D // 2
    f0 = np.exp(np.arange(half0, dtype=np.float32) * np.float32(-np.log(10000.0) / (half0 - 1)))
    f1 = np.exp(np.arange(half1, dtype=np.float32) * np.float32(-np.log(10000.0) / (half1 - 1)))
    consts = np.zeros((P, NCST), np.float32)
    consts[:, C_F0] = np.concatenate([f0, f0])
    consts[half0:, C_T0] = 0.25
    consts[half0:, C_O0] = TURN / 4
    consts[:, C_F1] = f1
    consts[:, C_EVEN] = np.arange(P) // DH % 2 == 0
    consts[:, C_ODD] = np.arange(P) // DH % 2 == 1

    x = a["x"]
    order = [head_at(n)[0] for n in range(H)]
    fside = a["fside_Bx16xSxS_0"][:, order].reshape(B, GROUPS, GH, NC, P, S).transpose(0, 1, 4, 2, 3, 5)
    l0, l1 = "L0_cond_", "L1_cond_"
    arrays = {
        "x_tok": x.reshape(B, NC, P, D).transpose(0, 2, 1, 3).reshape(B, P, NC * D),
        "x_feat": x.transpose(0, 2, 1).reshape(B, NC, P, S).transpose(0, 2, 1, 3).reshape(B, P, NC * S),
        "cond_t": a["condB_t"],
        "step_t": a["itok_B_34_63"],
        "fside": fside.reshape(B, GROUPS, P, GH, NC * S),
        "mask": a["mask_Bx1xSxS_bk0"].reshape(B, NC, P, S).transpose(0, 2, 1, 3).reshape(B, P, NC * S),
        "gbT": np.stack([rows_of(a[l0 + n].T) for n in ("gamma", "beta")], 1),
        "wmain": np.concatenate([rows_of(a[n]) for n in (
            l0 + "W_in", l0 + "W_out", l1 + "Wq", l1 + "Wk", l1 + "Wv", l1 + "Wo", l1 + "W1", l1 + "W2")], 1),
        "wcond": np.concatenate([rows_of(a[n]) for n in (
            l0 + "W1", l0 + "W2", l0 + "Wsc", l0 + "Wsh", l1 + "W_ada")], 1),
        "vecs": np.concatenate([columns(a[n]) for n in (
            l0 + "b1", l0 + "b2", l0 + "bsc", l0 + "bsh", l0 + "b_in", l1 + "b_ada", l1 + "bq", l1 + "bk",
            l1 + "b1", l1 + "g2", l1 + "beta2")], 1),
        "consts": consts,
        "rows": np.stack([a[l0 + "b_out"], a[l1 + "bv"], a[l1 + "bo"], a[l1 + "b2"]]),
    }
    nc = bacc.Bacc("TRN2", target_bir_lowering=False, num_devices=1)
    args, fed = [], {}
    for name, value in arrays.items():
        value = np.ascontiguousarray(value)
        fed[f"in_{name}"] = value
        args.append(nc.dram_tensor(f"in_{name}", value.shape, mybir.dt.from_np(value.dtype),
                                   kind="ExternalInput").ap())
    out = nc.dram_tensor("out", (B, P, NC * D), F32, kind="ExternalOutput").ap()
    build(nc, *args, out)
    got = run(nc, [fed], core_ids=[0]).results[0]["out"]
    return np.ascontiguousarray(got.reshape(B, P, NC, D).transpose(0, 2, 1, 3).reshape(B, S, D))
```

```python
from contextlib import ExitStack

import concourse.bass as bass
from concourse import mybir

F32 = mybir.dt.float32
F32R = mybir.dt.float32r
I32 = mybir.dt.int32
U8 = mybir.dt.uint8
ALU = mybir.AluOpType
ACT = mybir.ActivationFunctionType

P = 128
B, S, D = 8, 256, 256
H, DH = 16, 16
E = 128
HID = 4 * E
FF = 1024
NC = D // P
NF = FF // P
NH = HID // P
GROUPS, GH = 4, 4
EPS = 1e-5
MASKED = -1e30
HUGE = 3e38
MAGIC = 1.5 * 2 ** 23
TURN = 6.283185307179586
TURN1 = 6.28125
TURN2 = 2029 / 2 ** 20
TURN3 = TURN - TURN1 - TURN2
ARC = 3.1415925
SEED = 1597463007.0

COLS = {}
for _name, _n in (("b1", NH), ("b2", NH), ("bsc", NC), ("bsh", NC), ("b_in", NC), ("ada", 2 * NC),
                  ("bq", NC), ("bk", NC), ("bv", NC), ("bo", NC), ("ff1", NF), ("g2", NC), ("beta2", NC)):
    COLS[_name] = (sum(n for _, n in COLS.values()), _n)
NCOL = sum(n for _, n in COLS.values())
C_F0, C_T0, C_O0, C_F1, NCST = range(5)
WAT = {}
for _name, _k, _n in (("in", NC, D), ("out", NC, D), ("q", NC, D), ("k", NC, D), ("v", NC, D),
                      ("o", NC, D), ("ff1", NC, FF), ("ff2", NF, D)):
    WAT[_name] = (sum(k * n for _, k, n in WAT.values()), _k, _n)
NW = sum(k * n for _, k, n in WAT.values())
W_L0 = WAT["q"][0]
CAT = {}
for _name, _k, _n in (("w1", 1, HID), ("w2", NH, HID), ("wsc", NH, D), ("wsh", NH, D), ("wada", NC, 2 * D)):
    CAT[_name] = (sum(k * n for _, k, n in CAT.values()), _k, _n)
NCW = sum(k * n for _, k, n in CAT.values())
R_OUT, R_FF2, NROW = range(3)
HI, LO = range(2)
STACK = ((HI, LO, HI), (HI, HI, LO))
KROWS = 3 * DH
ACT_MOVES = (2, 5, 8, 11, 14)
LAG = 2
EARLY = 5


def moved(b, n):
    if isinstance(n, int) and n < 0:
        b, n = b - 1, n + 16
    by_act = n in ACT_MOVES
    each = len(ACT_MOVES) if by_act else 16 - len(ACT_MOVES)
    return by_act, b * each + sum((m in ACT_MOVES) == by_act for m in range(n + 1))


def head_at(n):
    g, band = divmod(n, GH)
    chunk, odd = divmod(g, 2)
    return 8 * chunk + 2 * band + odd, band, chunk, odd


def hold(engine):
    engine.nop(nofuse=True)


class Chain:

    def __init__(self, sem, per, held=False):
        self.sem, self.per, self.held = sem, per, held

    def start(self, b, at=0):
        self.b, self.at = b, at
        return self

    def link(self, engine, instruction):
        self.at += 1
        assert self.at <= self.per
        instruction.then_inc(self.sem, 1)
        engine.wait_ge(self.sem, self.b * self.per + self.at)
        if self.held:
            hold(engine)


def need(engine, sem, value):
    if not isinstance(value, int) or value > 0:
        engine.wait_ge(sem, value)


def build(nc, x_tok, x_feat, cond_t, step_t, fside, mask, gbT, wmain, wcond, vecs, consts, rows, out):
    with ExitStack() as ctx:
        def sb(name, shape, dt=F32):
            return ctx.enter_context(nc.sbuf_tensor(name, shape, dt))

        def psum(name):
            return ctx.enter_context(nc.psum_tensor(name, [P, 512], F32))

        def sem(name):
            return ctx.enter_context(nc.semaphore(name))

        w = sb("w", [P, NW])
        gb = sb("gb", [P, 2, NC * S])
        vec = sb("vec", [P, NCOL])
        cst = sb("cst", [P, NCST])
        brow = sb("brow", [P, NROW, D])
        ident = sb("ident", [P, P])
        mean_of = sb("mean_of", [P, P])
        tb = sb("tb", [P, B])
        tsi = sb("tsi", [P, B], I32)
        bns = sb("bns", [P, B, 6])
        bna = sb("bna", [P, B, 2])
        st1 = sb("st1", [P, 2, B])
        mean1 = sb("mean1", [P, B])
        rstd1 = sb("rstd1", [P, B])
        var1 = sb("var1", [P, B])
        angle = sb("angle", [P, 3, B])
        turns = sb("turns", [P, 3, B])
        emb = sb("emb", [P, 3, B])
        embh = sb("embh", [P, 3, B])
        h1 = sb("h1", [P, NH, B])
        h1t = sb("h1t", [P, NH, B])
        h2 = sb("h2", [P, NH, B])
        half_sc = sb("half_sc", [P, NC, B])
        half_sh = sb("half_sh", [P, NC, B])
        ada = sb("ada", [P, 2 * NC, B])
        bq4 = sb("bq4", [P, NC])
        bov = sb("bov", [P, NC])

        xt = sb("xt", [P, NC * D])
        xf = sb("xf", [P, NC * S])
        xb = sb("xb", [P, NC * D])
        lna = sb("lna", [P, NC * S])
        lny = sb("lny", [P, NC * S])
        qk_part = sb("qk_part", [P, 2, 2, NC * S], F32R)
        lnt = sb("lnt", [P, NC * S])
        hin = sb("hin", [P, NC * S])
        mid = sb("mid", [P, NC * S])
        mst = sb("mst", [P, 6])
        mag = sb("mag", [P, 2])
        mst2 = sb("mst2", [P, 2])
        x1 = sb("x1", [P, NC, D])
        xn = sb("xn", [P, NC * D])
        xaT = sb("xaT", [P, NC, S])
        xres = sb("xres", [P, NC, S])
        stack = sb("stack", [64, 2, H, S], F32R)
        parts = nc.dram_tensor("parts", [2, 2, P, NC * S], F32R).ap()
        vpad = sb("vpad", [P, NC, H, 2 * DH])
        m8 = sb("m8", [P, NC * S], U8)
        maskneg = sb("maskneg", [P, NC * S])
        bias = sb("bias", [P, GROUPS, GH, NC * S])
        sneg = sb("sneg", [P, 2, NC, S])
        negmax = sb("negmax", [P, NC, H])
        prob = sb("prob", [P, 2, NC, S])
        rsum = sb("rsum", [P, NC, H])
        rinv = sb("rinv", [P, NC, H])
        rinvx = sb("rinvx", [P, NC, H, DH])
        room2 = sb("room2", [P, 2 * GH * NC * S + NF * S])
        probT = room2[:, 0:2 * GH * NC * S].rearrange("p (n s) -> p n s", n=2 * GH)
        fT = room2[:, 2 * GH * NC * S:].rearrange("p (m s) -> p m s", m=NF)
        cw = room2
        rbc = sb("rbc", [P, NC * S])
        ctxT = sb("ctxT", [P, NC, S])
        x2 = sb("x2", [P, NC, D])
        x2b = sb("x2b", [P, NC * D])
        x2n = sb("x2n", [P, NC * D])
        hT = sb("hT", [P, NC, S])
        room = sb("room", [P, B, NC * S])
        uT = room[:, 0:NF // 2, :].rearrange("p a (m n) -> p (a m) n", m=2)
        uth = room[:, NF // 2:NF, :].rearrange("p a (m n) -> p (a m) n", m=2)
        xall = room
        outt = sb("outt", [P, NC * D])

        def newton_buffers(name, n):
            return {k: sb(f"{name}_{k}", [P, n], I32 if k in ("h", "s") else F32) for k in "vhsnar"} | {
                "bs": sb(f"{name}_bs", [P, NC, 6]), "ba": sb(f"{name}_ba", [P, NC, 2])}

        ln2, ln3, ln4 = (newton_buffers(f"ln{i}", n) for i, n in ((2, 1), (3, NC), (4, NC)))

        score = [psum("score0"), psum("score1")]
        trans = [psum("trans0"), psum("trans1")]
        context = psum("context")
        M0, M1, M2 = psum("M0"), psum("M1"), psum("M2")

        def W(name):
            at, k, n = WAT[name]
            return w[:, at:at + k * n].rearrange("p (k n) -> p k n", k=k)

        def CW(name):
            at, k, n = CAT[name]
            return cw[:, at:at + k * n].rearrange("p (k n) -> p k n", k=k)

        def col(name, i=0, n=1):
            return vec[:, COLS[name][0] + i:COLS[name][0] + i + n]

        def halves(t):
            return t[:, :].rearrange("p (c n) -> p c n", c=2)

        small_loaded, cond1_loaded, cond_loaded, xall_loaded, layer0_loaded, weights_loaded = map(
            sem, ("small_loaded", "cond1_loaded", "cond_loaded", "xall_loaded", "layer0_loaded", "weights_loaded"))
        scaled = sem("scaled")
        x_loaded, mask_loaded = sem("x_loaded"), sem("mask_loaded")
        bias_loaded = [sem(f"bias_loaded{g}") for g in range(GROUPS)]
        out_stored = sem("out_stored")
        ident_ready, zeros_ready = sem("ident_ready"), sem("zeros_ready")
        st1_ready, st1_done, var1_ready, std1_ready, angle_ready, emb_ready, embt_ready, embs_ready = map(
            sem, ("st1_ready", "st1_done", "var1_ready", "std1_ready", "angle_ready", "emb_ready",
                  "embt_ready", "embs_ready"))
        w1_done, h1_ready, h1t_ready, h1s_ready, w2_done, h2_ready, wsc_done, wada_done, bov_done, setup_ready, bov_ready = map(
            sem, ("w1_done", "h1_ready", "h1t_ready", "h1s_ready", "w2_done", "h2_ready", "wsc_done",
                  "wada_done", "bov_done", "setup_ready", "bov_ready"))
        v_setup, v_late = Chain(sem("v_setup"), 64), Chain(sem("v_late"), 1)
        bias_ready, qk_done, smax_done, exp_done, tr_done, pt_dve, pt_act = map(
            sem, ("bias_ready", "qk_done", "smax_done", "exp_done", "tr_done", "pt_dve", "pt_act"))
        pv_done = sem("pv_done")
        xb_ready, y_ready, tanh_ready, hin_ready, win_done, mid_ready = map(
            sem, ("xb_ready", "y_ready", "tanh_ready", "hin_ready", "win_done", "mid_ready"))
        mst_ready, mst_done, seed2, rs2, wout_done, x1_ready = map(
            sem, ("mst_ready", "mst_done", "seed2", "rs2", "wout_done", "x1_ready"))
        seed3, rs3, xn_ready, nt_done, xaT_ready, xres_ready = map(
            sem, ("seed3", "rs3", "xn_ready", "nt_done", "xaT_ready", "xres_ready"))
        q_done, k_done, v_done, hi_ready, lo_ready, parts_stored, stack_loaded0, stack_loaded1, v_ready = map(
            sem, ("q_done", "k_done", "v_done", "hi_ready", "lo_ready", "parts_stored",
                  "stack_loaded0", "stack_loaded1", "v_ready"))
        stack_loaded = (stack_loaded0, stack_loaded1)
        mask_ready, mask_read = sem("mask_ready"), sem("mask_read")
        rinv_ready, rinvx_ready, r_done, r_ready, ctx_ready, wo_done, x2_ready = map(
            sem, ("rinv_ready", "rinvx_ready", "r_done", "r_ready", "ctx_ready", "wo_done", "x2_ready"))
        seed4, rs4, x2b_ready, x2n_ready, n2t_done, hT_ready = map(
            sem, ("seed4", "rs4", "x2b_ready", "x2n_ready", "n2t_done", "hT_ready"))
        ff1_done, u_ready, uth_ready, f_ready, ff2_done, out_ready = map(
            sem, ("ff1_done", "u_ready", "uth_ready", "f_ready", "ff2_done", "out_ready"))
        v_apply, v_ln2a, v_ln2b, v_ln3, v_ln4 = (
            Chain(sem(n), k) for n, k in (("v_apply", 4), ("v_ln2a", 2), ("v_ln2b", 4), ("v_ln3", 4), ("v_ln4", 4)))
        p_rs2, p_rs3, p_rs4 = (Chain(sem(n), 6, True) for n in ("p_rs2", "p_rs3", "p_rs4"))

        def mm(pe, o, lhsT, rhs, start=True, stop=True):
            return nc.tensor.matmul(o, lhsT, rhs, start=start, stop=stop)

        block = ctx.enter_context(nc.Block())

        def turns_of_the_loop(engine, turn):
            turn(-2, False, False, True, False)
            turn(-1, False, True, True, False)
            turn(0, True, True, True, False)
            turn(1, True, True, True, True)
            with engine.Fori(2, B - 2) as b:
                turn(b, True, True, True, True)
            turn(B - 2, True, True, False, True)
            turn(B - 1, True, False, False, True)
            turn(B, False, False, False, True)

        @block.sync
        def _(sp):
            sp.dma_start(vec[:, :], vecs).then_inc(small_loaded, 16)
            sp.dma_start(cst[:, :], consts).then_inc(small_loaded, 16)
            sp.dma_start(tb[:, :], cond_t.partition_broadcast(P)).then_inc(small_loaded, 16)
            sp.dma_start(tsi[:, :], step_t.partition_broadcast(P)).then_inc(small_loaded, 16)
            sp.dma_start(cw[:, 0:HID], wcond[:, 0:HID]).then_inc(cond1_loaded, 16)
            sp.dma_start(cw[:, HID:NCW], wcond[:, HID:NCW]).then_inc(cond_loaded, 16)
            sp.dma_start(xall[:, :, :], x_feat.rearrange("b p n -> p b n")).then_inc(xall_loaded, 16)
            sp.dma_start(gb[:, :, :], gbT).then_inc(layer0_loaded, 16)
            sp.dma_start(w[:, 0:W_L0], wmain[:, 0:W_L0]).then_inc(layer0_loaded, 16)

            def load_x(b):
                need(sp, xb_ready, b)
                need(sp, v_apply.sem, 4 * b - 3)
                hold(sp)
                sp.dma_start(xf[:, :], x_feat[b, :, :]).then_inc(x_loaded, 16)
                sp.dma_start(xt[:, :], x_tok[b, :, :]).then_inc(x_loaded, 16)

            def load_bias(b, g):
                need(sp, smax_done, 16 * (b - 1) + GH * (g + 1))
                hold(sp)
                sp.dma_start(bias[:, g, :, :], fside[b, g, :, :]).then_inc(bias_loaded[g], 16)

            def restack(b, c):
                need(sp, qk_done, 16 * (b - 1) + 8 * (c + 1))
                hold(sp)
                for i in range(2):
                    for j, part in enumerate(STACK[i]):
                        sp.dma_start(
                            stack[DH * j:DH * (j + 1), i, 8 * c:8 * c + 8, :].bitcast(F32),
                            parts[i, part, :, c * S:(c + 1) * S].rearrange("(h d) s -> d h s", d=DH).bitcast(F32))\
                          .then_inc(stack_loaded[c], 16)

            def turn(b, att, proj, layer0, post):
                if proj:
                    need(sp, mask_ready, b + 1)
                    hold(sp)
                    sp.dma_start(m8[:, :], mask[b + 1, :, :]).then_inc(mask_loaded, 16)
                    load_bias(b + 1, 0)
                    load_bias(b + 1, 1)
                    for c in range(2):
                        need(sp, stack_loaded[c], 96 * b + 96)
                    for i in range(2):
                        sp.wait_ge(hi_ready, 2 * b + 3 + i)
                        sp.wait_ge(lo_ready, 2 * b + 3 + i)
                        hold(sp)
                        sp.dma_start(parts[i, :, :, :].rearrange("a p n -> p a n").bitcast(F32),
                                     qk_part[:, i, :, :].bitcast(F32)).then_inc(parts_stored, 16)
                    sp.wait_ge(parts_stored, 32 * b + 64)
                    restack(b + 1, 0)
                    load_bias(b + 1, 2)
                if layer0 and not (isinstance(b, int) and b == B - 3):
                    load_x(b + 3)
                if proj:
                    load_bias(b + 1, 3)
                    restack(b + 1, 1)
                if post:
                    sp.wait_ge(out_ready, b)
                    hold(sp)
                    sp.dma_start(out[b - 1, :, :], outt[:, :]).then_inc(out_stored, 16)

            load_x(0)
            sp.dma_start(brow[:, :, :], rows.partition_broadcast(P)).then_inc(weights_loaded, 16)
            sp.dma_start(w[:, W_L0:NW], wmain[:, W_L0:NW]).then_inc(weights_loaded, 16)
            turn(-2, False, False, True, False)
            turn(-1, False, True, True, False)
            turn(0, True, True, True, False)
            turn(1, True, True, True, True)
            with sp.Fori(2, B - 3) as b:
                turn(b, True, True, True, True)
            turn(B - 3, True, True, True, True)
            turn(B - 2, True, True, False, True)
            turn(B - 1, True, False, False, True)
            turn(B, False, False, False, True)
            sp.wait_ge(out_stored, 16 * B)

        @block.gpsimd
        def _(pool):
            nc.gpsimd.memset(ident[:, :], 0.0).then_inc(zeros_ready, 1)
            nc.gpsimd.memset(mean_of[:, :], 1.0 / P).then_inc(ident_ready, 1)
            nc.gpsimd.memset(vpad[:, :, :, :], 0.0).then_inc(ident_ready, 1)
            pool.wait_ge(zeros_ready, 1)
            nc.gpsimd.affine_select(out=ident[:, :], in_=ident[:, :], compare_op=ALU.not_equal, fill=1.0,
                                    base=0, pattern=[[-1, P]], channel_multiplier=1).then_inc(ident_ready, 1)

            def rsqrt(b, chain, t, n, seeded, done):
                c = chain.start(b)
                pool.wait_ge(seeded, b + 1)
                hold(pool)
                c.link(pool, nc.gpsimd.tensor_scalar(t["n"][:, :], t["v"][:, :], -0.5, None, ALU.mult))
                r = t["s"][:, :].bitcast(F32)
                for i in range(3):
                    for j in range(n):
                        a = nc.gpsimd.tensor_scalar(t["a"][:, j:j + 1], r[:, j:j + 1], r[:, j:j + 1],
                                                    t["n"][:, j:j + 1], ALU.mult, ALU.mult)
                    c.link(pool, a)
                    for j in range(n):
                        a = nc.gpsimd.tensor_scalar(t["r"][:, j:j + 1], t["a"][:, j:j + 1], 1.5,
                                                    r[:, j:j + 1], ALU.add, ALU.mult)
                    if i < 2:
                        c.link(pool, a)
                    r = t["r"][:, :]
                a.then_inc(done, 1)

            def mask_heads(b, g, heads):
                if 0 in heads:
                    pool.wait_ge(bias_loaded[g], 16 * b + 16)
                for i in heads:
                    nc.gpsimd.tensor_tensor(bias[:, g, i, :], bias[:, g, i, :], maskneg[:, :],
                                            ALU.add).then_inc(bias_ready, 1)

            pool.wait_ge(weights_loaded, 32)
            nc.gpsimd.tensor_scalar(W("q"), W("q"), DH ** -0.5, None, ALU.mult).then_inc(scaled, 1)
            nc.gpsimd.tensor_scalar(W("ff2"), W("ff2"), 0.5, None, ALU.mult).then_inc(scaled, 1)

            def mask_out(b):
                pool.wait_ge(mask_loaded, 16 * b + 16)
                need(pool, bias_ready, 16 * b)
                hold(pool)
                nc.gpsimd.tensor_scalar(maskneg[:, :], m8[:, :], MASKED, None, ALU.mult).then_inc(mask_ready, 1)
                pool.wait_ge(mask_ready, b + 1)

            def turn(b, att, proj, layer0, post):
                n1, n2 = b + 1, b + 2
                if proj and not att:
                    mask_out(n1)
                    for g in (0, 1):
                        mask_heads(n1, g, range(GH))
                if att:
                    for g in (2, 3):
                        mask_heads(b, g, range(GH))
                if post:
                    rsqrt(b - 1, p_rs4, ln4, NC, seed4, rs4)
                if layer0:
                    rsqrt(n2, p_rs2, ln2, 1, seed2, rs2)
                if post:
                    need(pool, out_ready, b - 1)
                    nc.gpsimd.tensor_tensor(halves(x2b), x2[:, :, :],
                                            brow[:, R_FF2, :].unsqueeze(1).to_broadcast([P, NC, D]),
                                            ALU.add).then_inc(x2b_ready, 1)
                if layer0:
                    need(pool, x1_ready, n2)
                    pool.wait_ge(x_loaded, 32 * n2 + 32)
                    nc.gpsimd.tensor_tensor(halves(xb), halves(xt),
                                            brow[:, R_OUT, :].unsqueeze(1).to_broadcast([P, NC, D]),
                                            ALU.add).then_inc(xb_ready, 1)
                if proj and att:
                    mask_out(n1)
                    mask_heads(n1, 0, range(GH))
                if layer0:
                    rsqrt(n2, p_rs3, ln3, NC, seed3, rs3)
                if proj and att:
                    mask_heads(n1, 1, range(GH))

            turns_of_the_loop(pool, turn)

        @block.tensor
        def _(pe):
            pe.wait_ge(ident_ready, 3)
            pe.wait_ge(cond1_loaded, 16)
            pe.wait_ge(emb_ready, 1)
            for m in range(NH):
                last = mm(pe, M0[:, m * B:(m + 1) * B], CW("w1")[:, 0, m * P:(m + 1) * P], emb[:, 0, :])
            last.then_inc(w1_done, 1)
            pe.wait_ge(cond_loaded, 16)
            pe.wait_ge(h1s_ready, 1)
            for m in range(NH):
                for k in range(NH):
                    last = mm(pe, M1[:, m * B:(m + 1) * B], CW("w2")[:, k, m * P:(m + 1) * P], h1[:, k, :],
                              k == 0, k == NH - 1)
            last.then_inc(w2_done, 1)
            pe.wait_ge(h2_ready, 1)
            for j, name in enumerate(("wsc", "wsh")):
                for m in range(NC):
                    for k in range(NH):
                        at = (j * NC + m) * B
                        last = mm(pe, M0[:, at:at + B], CW(name)[:, k, m * P:(m + 1) * P], h2[:, k, :],
                                  k == 0, k == NH - 1)
            last.then_inc(wsc_done, 1)
            pe.wait_ge(st1_ready, 1)
            mm(pe, M2[:, 0:2 * B], mean_of[:, :], st1[:, :, :]).then_inc(st1_done, 1)
            pe.wait_ge(embs_ready, 1)
            pe.wait_ge(h2_ready, 1)
            for m in range(2 * NC):
                for k in range(NC):
                    last = mm(pe, M1[:, m * B:(m + 1) * B], CW("wada")[:, k, m * P:(m + 1) * P],
                              embh[:, 1 + k, :], k == 0, k == NC - 1)
            last.then_inc(wada_done, 1)
            pe.wait_ge(layer0_loaded, 32)

            def scores(b, n):
                h, band, c, odd = head_at(n)
                if n % 8 == 0:
                    pe.wait_ge(stack_loaded[c], 96 * b + 96)
                need(pe, smax_done, 16 * b + n - 1)
                for t in range(NC):
                    last = mm(pe, score[n % 2][:, t * S:(t + 1) * S], stack[0:KROWS, 0, h, t * P:(t + 1) * P],
                              stack[0:KROWS, 1, h, :])
                last.then_inc(qk_done, 1)

            def turned_out(b, n):
                by_act, count = moved(b, n)
                need(pe, pt_act if by_act else pt_dve, count)

            def turn_probs(b, n):
                pe.wait_ge(exp_done, 16 * b + n + 1)
                turned_out(b, n - 2)
                for k in range(NC):
                    for t in range(NC):
                        last = nc.tensor.transpose(trans[n % 2][:, k * S + t * P:k * S + (t + 1) * P],
                                                   prob[:, n % 2, t, k * P:(k + 1) * P], ident[:, :])
                last.then_inc(tr_done, 1)

            def values(b, g):
                for n in range(GH * g, GH * (g + 1)):
                    if n + 1 == GH * (g + 1) or moved(0, n)[0] != moved(0, GH * g + GH - 1)[0]:
                        turned_out(b, n)
                pe.wait_ge(v_ready, b + 1)
                if g == 0:
                    need(pe, ctx_ready, b)
                for k in range(NC):
                    for i in range(GH):
                        h, band, c, odd = head_at(GH * g + i)
                        last = mm(pe, context[32 * band:32 * band + 32, c * S:(c + 1) * S], vpad[:, k, h, :],
                                  probT[:, (g % 2) * GH + i, k * S:(k + 1) * S],
                                  k == 0 and odd == 0, k == NC - 1 and odd == 1)
                last.then_inc(pv_done, 1)

            def features_out(bank, name, src):
                for m in range(NC):
                    for k in range(NC):
                        last = mm(pe, bank[:, m * S:(m + 1) * S], W(name)[:, k, m * P:(m + 1) * P], src[:, k, :],
                                  k == 0, k == NC - 1)
                return last

            def tokens_out(bank, name, src, add=None):
                for t in range(NC):
                    for k in range(NC):
                        last = mm(pe, bank[:, t * D:(t + 1) * D], src[:, k, t * P:(t + 1) * P], W(name)[:, k, :],
                                  k == 0, k == NC - 1)
                    if add is not None:
                        for c in range(NC):
                            last = nc.tensor.matmul(bank[:, t * D + c * P:t * D + (c + 1) * P],
                                                    add[:, c, t * P:(t + 1) * P], ident[:, :],
                                                    start=False, stop=True, is_transpose=True,
                                                    skip_group_check=True)
                return last

            def turned(bank, src):
                for c in range(NC):
                    for t in range(NC):
                        last = nc.tensor.transpose(bank[:, c * S + t * P:c * S + (t + 1) * P],
                                                   src[:, t * D + c * P:t * D + (c + 1) * P], ident[:, :])
                return last

            def ff1(b, j, bank):
                pe.wait_ge(hT_ready, 2 * b)
                for i in range(2):
                    m = 2 * j + i
                    for k in range(NC):
                        last = mm(pe, bank[:, i * S:(i + 1) * S], W("ff1")[:, k, m * P:(m + 1) * P], hT[:, k, :],
                                  k == 0, k == NC - 1)
                last.then_inc(ff1_done, 1)

            def ff2(b, t, ks):
                for k in ks:
                    last = mm(pe, M1[:, t * D:(t + 1) * D], fT[:, k, t * P:(t + 1) * P], W("ff2")[:, k, :],
                              k == 0, k == NF - 1)
                return last

            def bov_product():
                pe.wait_ge(weights_loaded, 32)
                pe.wait_ge(setup_ready, 1)
                pe.wait_ge(small_loaded, 64)
                for m in range(NC):
                    for k in range(NC):
                        last = mm(pe, M1[:, m:m + 1], W("o")[:, k, m * P:(m + 1) * P],
                                  col("bv", k), k == 0, k == NC - 1)
                last.then_inc(bov_done, 1)

            def filler(b, s, att, proj, layer0, post):
                n1, n2 = b + 1, b + 2
                p = s if att else s + EARLY
                if s == 0 and proj and not att:
                    bov_product()
                if s == 1 and att:
                    need(pe, out_ready, b - 1)
                    pe.wait_ge(xaT_ready, 2 * b + 2)
                    tokens_out(M1, "v", xaT).then_inc(v_done, 1)
                if s == 1 and post:
                    need(pe, lo_ready, 2 * b + 2 if att else 0)
                    need(pe, u_ready, 8 * b - 8)
                    pe.wait_ge(rinvx_ready, b)
                    for c in range(NC):
                        for t in range(NC):
                            last = nc.tensor.transpose(
                                M2[:, c * S + t * P:c * S + (t + 1) * P],
                                rinvx[:, t, 8 * c:8 * c + 8, :].rearrange("p h d -> p (h d)"), ident[:, :])
                    last.then_inc(r_done, 1)
                if s == 3 and layer0:
                    pe.wait_ge(hin_ready, 2 * n2 + 1)
                    need(pe, x1_ready, n2)
                    if proj and not att:
                        pe.wait_ge(lo_ready, 2 * n1 + 2)
                    features_out(M0, "in", halves(hin)).then_inc(win_done, 1)
                if s == 4 and post:
                    pe.wait_ge(ctx_ready, b)
                    if att:
                        pe.wait_ge(v_ready, b + 1)
                    else:
                        pe.wait_ge(out_ready, b - 1)
                    pe.wait_ge(xres_ready, 2 * b)
                    tokens_out(M1, "o", ctxT, xres).then_inc(wo_done, 1)
                if s == 5 and layer0:
                    pe.wait_ge(mst_ready, n2 + 1)
                    need(pe, lo_ready, 2 * b + 2 if att else 2 * n1 + 2 if proj else 0)
                    need(pe, r_ready, b if post else 0)
                    need(pe, u_ready, 8 * b - 8 if post else 0)
                    mm(pe, M2[:, 0:2], mean_of[:, :], mag[:, :]).then_inc(mst_done, 1)
                if p == 5 and proj:
                    pe.wait_ge(xn_ready, n1 + 1)
                    if layer0 and att:
                        pe.wait_ge(mid_ready, 2 * n2 + 2)
                    turned(M0, xn).then_inc(nt_done, 1)
                if p == 6 and proj:
                    pe.wait_ge(xaT_ready, 2 * n1 + 2)
                    pe.wait_ge(scaled, 2)
                    if layer0 and att:
                        pe.wait_ge(v_ln2b.sem, 4 * n2 + 1)
                    need(pe, lo_ready, 2 * n1)
                    need(pe, r_ready, b)
                    need(pe, u_ready, 8 * b - 8)
                    features_out(M2, "q", xaT).then_inc(q_done, 1)
                if p == 7 and proj:
                    features_out(M0, "k", xaT).then_inc(k_done, 1)
                if s == 8 and post:
                    pe.wait_ge(x2n_ready, b)
                    turned(M1, x2n).then_inc(n2t_done, 1)
                if s == 11 and layer0:
                    pe.wait_ge(hin_ready, 2 * n2 + 2)
                    pe.wait_ge(mid_ready, 2 * n2 + 2)
                    need(pe, lo_ready, 2 * n1 + 2 if proj else 0)
                    tokens_out(M0, "out", halves(hin)).then_inc(wout_done, 1)
                if s in (9, 10, 11, 12) and post:
                    j = s - 9
                    if j == 1:
                        need(pe, lo_ready, 2 * n1 + 1 if proj else 0)
                        pe.wait_ge(r_ready, b)
                    if j >= 2:
                        pe.wait_ge(u_ready, 8 * b - 8 + 2 * (j - 1))
                    ff1(b, j, (M1, M2)[j % 2])
                for t, part in {13: ((0, 0),), 14: ((0, 1), (1, 0)), 15: ((1, 1),)}.get(s, ()) if post else ():
                    if t == 0:
                        pe.wait_ge(f_ready, 4 * b - 2 + 2 * part)
                    pe.wait_ge(u_ready, 8 * b - 2)
                    last = ff2(b, t, range(part * NF // 2, (part + 1) * NF // 2))
                    if s == 15:
                        last.then_inc(ff2_done, 1)

            def turn(b, att, proj, layer0, post):
                for s in range(16):
                    if att:
                        scores(b, s)
                    if s < LAG:
                        if post:
                            turn_probs(b - 1, s - LAG + 16)
                    elif att:
                        turn_probs(b, s - LAG)
                    filler(b, s, att, proj, layer0, post)
                    if s == LAG and post:
                        values(b - 1, GROUPS - 1)
                    if att and s % GH == LAG and s > LAG:
                        values(b, s // GH - 1)

            turns_of_the_loop(pe, turn)

        @block.scalar
        def _(act):
            act.wait_ge(angle_ready, 1)
            nc.scalar.activation(emb[:, :, :], angle[:, :, :], ACT.Sin).then_inc(emb_ready, 1)
            act.wait_ge(emb_ready, 1)
            nc.scalar.activation(embh[:, :, :], emb[:, :, :], ACT.Tanh, scale=0.5).then_inc(embt_ready, 1)
            act.wait_ge(h1_ready, 1)
            nc.scalar.activation(h1t[:, :, :], h1[:, :, :], ACT.Tanh, scale=0.5).then_inc(h1t_ready, 1)
            act.wait_ge(var1_ready, 1)
            nc.scalar.activation(rstd1[:, :], var1[:, :], ACT.Sqrt).then_inc(std1_ready, 1)

            def exps(b, n):
                h = head_at(n)[0]
                act.wait_ge(smax_done, 16 * b + n + 1)
                need(act, tr_done, 16 * b + n - 1)
                if n == 0:
                    need(act, rinv_ready, b)
                for t in range(NC):
                    last = nc.scalar.activation(prob[:, n % 2, t, :], sneg[:, n % 2, t, :], ACT.Exp,
                                                bias=negmax[:, t, h:h + 1], scale=-1.0,
                                                accum_out=rsum[:, t, h:h + 1])
                last.then_inc(exp_done, 1)

            def tanh_of(b, k):
                act.wait_ge(y_ready, 2 * b + 1 + k)
                need(act, hin_ready, 2 * b + k)
                nc.scalar.activation(lnt[:, :], lny[:, :], ACT.Tanh).then_inc(tanh_ready, 1)

            def filler(b, s, att, proj, layer0, post):
                n1, n2 = b + 1, b + 2
                p = s if att else s + EARLY
                if s == 1 and post:
                    act.wait_ge(r_done, b)
                    need(act, ctx_ready, b - 1)
                    nc.scalar.activation(rbc[:, :], M2[:, :], ACT.Copy).then_inc(r_ready, 1)
                if s == 2 and att:
                    act.wait_ge(v_done, b + 1)
                    need(act, pv_done, 4 * b)
                    for odd in range(2):
                        src = M1[:, :].rearrange("p (t h o d) -> p t h o d", t=NC, o=2, d=DH)
                        dst = vpad[:, :, :, odd * DH:(odd + 1) * DH].rearrange("p t (h o) d -> p t h o d", o=2)
                        last = nc.scalar.activation(dst[:, :, :, odd, :], src[:, :, :, odd, :], ACT.Copy)
                    last.then_inc(v_ready, 1)
                if s == 1 and layer0:
                    tanh_of(n2, 0)
                if s == 4 and post:
                    act.wait_ge(wo_done, b)
                    need(act, x2b_ready, b - 1)
                    nc.scalar.activation(x2[:, :, :], halves(M1), ACT.Copy).then_inc(x2_ready, 1)
                if s == 4 and att:
                    act.wait_ge(xaT_ready, 2 * b + 2)
                    act.wait_ge(bov_ready, 1)
                    need(act, wo_done, b)
                    for c in range(NC):
                        nc.scalar.activation(xres[:, c, :], xaT[:, c, :], ACT.Identity,
                                             bias=bov[:, c:c + 1]).then_inc(xres_ready, 1)
                if p == 5 and proj:
                    if not att:
                        act.wait_ge(setup_ready, 1)
                    act.wait_ge(nt_done, n1 + 1)
                    if att:
                        act.wait_ge(v_done, b + 1)
                        act.wait_ge(xres_ready, 2 * b + 2)
                    for c in range(NC):
                        at = ada[:, NC + c, bass.ds(n1, 1)]
                        nc.scalar.activation(xaT[:, c, :], M0[:, c * S:(c + 1) * S], ACT.Identity,
                                             bias=at, scale=ada[:, c, bass.ds(n1, 1)]).then_inc(xaT_ready, 1)
                if s == 3 and layer0:
                    act.wait_ge(win_done, n2 + 1)
                    for m in range(NC):
                        nc.scalar.activation(mid[:, m * S:(m + 1) * S], M0[:, m * S:(m + 1) * S], ACT.Identity,
                                             bias=col("b_in", m)).then_inc(mid_ready, 1)
                if p in (6, 7) and proj:
                    i = p - 6
                    bank = (M2, M0)[i]
                    act.wait_ge((q_done, k_done)[i], n1 + 1)
                    need(act, parts_stored, 32 * n1)
                    need(act, lo_ready, 2 * n1)
                    for c in range(NC):
                        last = nc.scalar.activation(qk_part[:, i, HI, c * S:(c + 1) * S], bank[:, c * S:(c + 1) * S],
                                                    ACT.Identity, bias=bq4[:, c:c + 1] if i == 0 else col("bk", c))
                    last.then_inc(hi_ready, 1)
                if s == 9 and layer0:
                    tanh_of(n2, 1)
                if s == 8 and post:
                    act.wait_ge(n2t_done, b)
                    for c in range(NC):
                        nc.scalar.activation(hT[:, c, :], M1[:, c * S:(c + 1) * S], ACT.Identity,
                                             bias=col("beta2", c), scale=col("g2", c)).then_inc(hT_ready, 1)
                if s in (9, 10, 11, 12) and post:
                    j = s - 9
                    act.wait_ge(ff1_done, 4 * b - 4 + j + 1)
                    bank = (M1, M2)[j % 2]
                    need(act, f_ready, 4 * (b - 1))
                    for i in range(2):
                        m = 2 * j + i
                        nc.scalar.activation(uT[:, m, :], bank[:, i * S:(i + 1) * S], ACT.Identity,
                                             bias=col("ff1", m)).then_inc(u_ready, 1)
                    act.wait_ge(u_ready, 8 * b - 8 + 2 * (j + 1))
                    nc.scalar.activation(uth[:, 2 * j:2 * j + 2, :], uT[:, 2 * j:2 * j + 2, :], ACT.Tanh,
                                         scale=0.5 * 1.702).then_inc(uth_ready, 1)

            def move(b, n):
                act.wait_ge(tr_done, 16 * b + n + 1)
                need(act, pv_done, 4 * b + n // GH - 1)
                nc.scalar.activation(probT[:, n % 8, :], trans[n % 2][:, :], ACT.Copy).then_inc(pt_act, 1)

            def turn(b, att, proj, layer0, post):
                for s in range(16):
                    if att:
                        exps(b, s)
                    if (att if s >= LAG else post) and (s - LAG) % 16 in ACT_MOVES:
                        move(b - (s < LAG), (s - LAG) % 16)
                    filler(b, s, att, proj, layer0, post)

            turns_of_the_loop(act, turn)

        @block.vector
        def _(dve):
            v = nc.vector
            c = v_setup.start(0)

            dve.wait_ge(small_loaded, 64)
            v.tensor_scalar(tb[:, :], tb[:, :], 5000.0, None, ALU.mult)
            c.link(dve, v.tensor_copy(angle[:, 2, :], tsi[:, :]))
            c.link(dve, v.tensor_scalar(angle[:, 2, :], angle[:, 2, :], 0.01, 4000.0, ALU.mult, ALU.mult))
            v.tensor_scalar(angle[:, 0, :], tb[:, :], cst[:, C_F0:C_F0 + 1], None, ALU.mult)
            v.tensor_scalar(angle[:, 1, :], angle[:, 2, :], cst[:, C_F1:C_F1 + 1], None, ALU.mult)
            c.link(dve, v.tensor_scalar(angle[:, 2, :], angle[:, 2, :], cst[:, C_F1:C_F1 + 1], None, ALU.mult))
            v.tensor_scalar(turns[:, 0, :], angle[:, 0, :], 1 / TURN, cst[:, C_T0:C_T0 + 1], ALU.mult, ALU.add)
            v.tensor_scalar(turns[:, 1, :], angle[:, 1, :], 1 / TURN, None, ALU.mult)
            c.link(dve, v.tensor_scalar(turns[:, 2, :], angle[:, 2, :], 1 / TURN, 0.25, ALU.mult, ALU.add))
            c.link(dve, v.tensor_scalar(turns[:, :, :], turns[:, :, :], MAGIC, None, ALU.add))
            c.link(dve, v.tensor_scalar(turns[:, :, :], turns[:, :, :], MAGIC, None, ALU.subtract))
            for part in (TURN1, TURN2, TURN3):
                c.link(dve, v.scalar_tensor_tensor(out=angle[:, :, :], in0=turns[:, :, :], scalar=-part,
                                                   in1=angle[:, :, :], op0=ALU.mult, op1=ALU.add))
            v.tensor_scalar(angle[:, 0, :], angle[:, 0, :], cst[:, C_O0:C_O0 + 1], None, ALU.add)
            c.link(dve, v.tensor_scalar(angle[:, 2, :], angle[:, 2, :], TURN / 4, None, ALU.add))
            v.tensor_scalar(angle[:, :, :], angle[:, :, :], ARC, -ARC, ALU.min, ALU.max).then_inc(angle_ready, 1)

            def silu(t, x):
                c.link(dve, v.scalar_tensor_tensor(out=x, in0=t, scalar=1.0, in1=x, op0=ALU.add, op1=ALU.mult))
                return v.tensor_scalar(x, x, 0.5, None, ALU.mult)

            def plus_col(o, x, name, n):
                return v.tensor_tensor(o, x, col(name, 0, n).unsqueeze(2).to_broadcast([P, n, B]), ALU.add)

            def small(bank, at, n):
                return bank[:, at * B:(at + n) * B].rearrange("p (m b) -> p m b", b=B)

            dve.wait_ge(w1_done, 1)
            plus_col(h1[:, :, :], small(M0, 0, NH), "b1", NH).then_inc(h1_ready, 1)
            dve.wait_ge(embt_ready, 1)
            c.link(dve, v.scalar_tensor_tensor(out=embh[:, :, :], in0=embh[:, :, :], scalar=1.0,
                                               in1=emb[:, :, :], op0=ALU.add, op1=ALU.mult))
            v.tensor_scalar(embh[:, :, :], embh[:, :, :], 0.5, None, ALU.mult).then_inc(embs_ready, 1)
            dve.wait_ge(h1t_ready, 1)
            silu(h1t[:, :, :], h1[:, :, :]).then_inc(h1s_ready, 1)
            dve.wait_ge(w2_done, 1)
            plus_col(h2[:, :, :], small(M1, 0, NH), "b2", NH).then_inc(h2_ready, 1)
            dve.wait_ge(xall_loaded, 16)
            for i in range(B):
                last = v.bn_stats(bns[:, i, :], xall[:, i, :])
            c.link(dve, last)
            for i in range(B):
                last = v.bn_aggr(bna[:, i, :], bns[:, i, :])
            c.link(dve, last)
            v.tensor_copy(st1[:, 0, :], bna[:, :, 0])
            c.link(dve, v.tensor_tensor(st1[:, 1, :], bna[:, :, 0], bna[:, :, 0], ALU.mult))
            v.tensor_tensor(st1[:, 1, :], st1[:, 1, :], bna[:, :, 1], ALU.add).then_inc(st1_ready, 1)
            dve.wait_ge(wsc_done, 1)
            plus_col(half_sc[:, :, :], small(M0, 0, NC), "bsc", NC)
            c.link(dve, plus_col(half_sh[:, :, :], small(M0, NC, NC), "bsh", NC))
            v.tensor_scalar(half_sc[:, :, :], half_sc[:, :, :], 0.5, None, ALU.mult)
            c.link(dve, v.tensor_scalar(half_sh[:, :, :], half_sh[:, :, :], 0.5, None, ALU.mult))
            dve.wait_ge(st1_done, 1)
            c.link(dve, v.tensor_copy(mean1[:, :], M2[:, 0:B]))
            c.link(dve, v.tensor_tensor(var1[:, :], mean1[:, :], mean1[:, :], ALU.mult))
            c.link(dve, v.scalar_tensor_tensor(out=var1[:, :], in0=var1[:, :], scalar=-1.0, in1=M2[:, B:2 * B],
                                               op0=ALU.mult, op1=ALU.add))
            v.tensor_scalar(var1[:, :], var1[:, :], EPS, None, ALU.add).then_inc(var1_ready, 1)
            dve.wait_ge(std1_ready, 1)
            c.link(dve, v.reciprocal(rstd1[:, :], rstd1[:, :]))
            dve.wait_ge(layer0_loaded, 32)

            def late_setup():
                c = v_late.start(0)
                dve.wait_ge(wada_done, 1)
                c.link(dve, plus_col(ada[:, :, :], small(M1, 0, 2 * NC), "ada", 2 * NC))
                v.tensor_scalar(ada[:, 0:NC, :], ada[:, 0:NC, :], 1.0, None, ALU.add)
                v.tensor_scalar(bq4[:, :], col("bq", 0, NC), DH ** -0.5, None, ALU.mult)\
                 .then_inc(setup_ready, 1)
                dve.wait_ge(bov_done, 1)
                v.tensor_tensor(bov[:, :], M1[:, 0:NC], col("bo", 0, NC), ALU.add).then_inc(bov_ready, 1)

            def softmax_max(b, n):
                h = head_at(n)[0]
                dve.wait_ge(qk_done, 16 * b + n + 1)
                dve.wait_ge(bias_ready, 16 * b + n + 1)
                need(dve, exp_done, 16 * b + n - 1)
                for t in range(NC):
                    if t == 0:
                        hold(dve)
                    last = v.tensor_tensor_reduce(
                        out=sneg[:, n % 2, t, :], in0=score[n % 2][:, t * S:(t + 1) * S],
                        in1=bias[:, n // GH, n % GH, t * S:(t + 1) * S], scale=-1.0, scalar=HUGE,
                        op0=ALU.add, op1=ALU.min, accum_out=negmax[:, t, h:h + 1])
                last.then_inc(smax_done, 1)

            def probs_out(b, n):
                dve.wait_ge(tr_done, 16 * b + n + 1)
                need(dve, pv_done, 4 * b + n // GH - 1)
                v.tensor_copy(probT[:, n % 8, :], trans[n % 2][:, :]).then_inc(pt_dve, 1)

            def apply(b, k, src, mean, rstd):
                c = v_apply.start(b, 2 * k)
                need(dve, hin_ready, 2 * b + k)
                c.link(dve, v.scalar_tensor_tensor(out=lna[:, :], in0=src, scalar=mean, in1=gb[:, 0, :],
                                                   op0=ALU.subtract, op1=ALU.mult))
                c.link(dve, v.scalar_tensor_tensor(out=lna[:, :], in0=lna[:, :], scalar=rstd, in1=gb[:, 1, :],
                                                   op0=ALU.mult, op1=ALU.add))
                for m in range(NC):
                    last = v.tensor_scalar(lny[:, m * S:(m + 1) * S], lna[:, m * S:(m + 1) * S],
                                           half_sc[:, m, bass.ds(b, 1)], half_sh[:, m, bass.ds(b, 1)],
                                           ALU.mult, ALU.add)
                last.then_inc(y_ready, 1)

            def silu_out(b, k):
                dve.wait_ge(tanh_ready, 2 * b + 1 + k)
                if k == 0:
                    need(dve, wout_done, b)
                else:
                    dve.wait_ge(win_done, b + 1)
                v.scalar_tensor_tensor(out=hin[:, :], in0=lnt[:, :], scalar=1.0, in1=lny[:, :],
                                       op0=ALU.add, op1=ALU.mult).then_inc(hin_ready, 1)

            def seed(b, c, t, seeded):
                c.link(dve, v.tensor_scalar(t["h"][:, :], t["v"][:, :].bitcast(I32), 1, None,
                                            ALU.arith_shift_right))
                v.tensor_scalar(t["s"][:, :], t["h"][:, :], -1.0, SEED, ALU.mult, ALU.add).then_inc(seeded, 1)

            def token_stats(b, chain, t, x, seeded):
                c = chain.start(b)
                for i in range(NC):
                    last = v.bn_stats(t["bs"][:, i, :], x[:, i, :])
                c.link(dve, last)
                hold(dve)
                for i in range(NC):
                    last = v.bn_aggr(t["ba"][:, i, :], t["bs"][:, i, :])
                c.link(dve, last)
                c.link(dve, v.tensor_scalar(t["v"][:, :], t["ba"][:, :, 1], EPS, None, ALU.add))
                seed(b, c, t, seeded)

            def token_norm(o, x, t):
                for i in range(NC):
                    last = v.tensor_scalar(o[:, i * D:(i + 1) * D], x[:, i, :], t["ba"][:, i, 0:1],
                                           t["r"][:, i:i + 1], ALU.subtract, ALU.mult)
                return last

            def before(b, s, att, proj, layer0, post):
                n1, n2 = b + 1, b + 2
                p = s if att else s + EARLY
                if s == 0 and proj and not att:
                    late_setup()
                if s == 0 and post:
                    dve.wait_ge(exp_done, 16 * b)
                    v.reciprocal(rinv[:, :, :], rsum[:, :, :]).then_inc(rinv_ready, 1)
                    dve.wait_ge(rinv_ready, b)
                    need(dve, r_done, b - 1)
                    v.tensor_copy(rinvx[:, :, :, :], rinv[:, :, :].unsqueeze(3).to_broadcast([P, NC, H, DH]))\
                     .then_inc(rinvx_ready, 1)
                if s == 2 and layer0:
                    silu_out(n2, 0)
                if s == 5 and post:
                    dve.wait_ge(x2_ready, b)
                    token_stats(b - 1, v_ln4, ln4, x2, seed4)
                if p in (7, 8) and proj:
                    i = p - 7
                    dve.wait_ge(hi_ready, 2 * n1 + 1 + i)
                    need(dve, parts_stored, 32 * n1)
                    for c in range(NC):
                        at = slice(c * S, (c + 1) * S)
                        last = v.scalar_tensor_tensor(out=qk_part[:, i, LO, at], in0=(M2, M0)[i][:, at],
                                                      scalar=bq4[:, c:c + 1] if i == 0 else col("bk", c),
                                                      in1=qk_part[:, i, HI, at].bitcast(F32),
                                                      op0=ALU.add, op1=ALU.subtract)
                    last.then_inc(lo_ready, 1)
                if s == 8 and post:
                    dve.wait_ge(rs4, b)
                    token_norm(x2n, x2, ln4).then_inc(x2n_ready, 1)
                if s == 8 and layer0:
                    dve.wait_ge(rs2, n2 + 1)
                    apply(n2, 1, mid[:, :], mst2[:, 0:1], ln2["r"][:, 0:1])
                if s == 10 and layer0:
                    silu_out(n2, 1)
                if s == 12 and layer0:
                    dve.wait_ge(wout_done, n2 + 1)
                    dve.wait_ge(xb_ready, n2 + 1)
                    v.tensor_tensor(x1[:, :, :], halves(M0), halves(xb), ALU.add).then_inc(x1_ready, 1)
                    dve.wait_ge(x1_ready, n2 + 1)
                    token_stats(n2, v_ln3, ln3, x1, seed3)

            def after(b, s, att, proj, layer0, post):
                n1, n2 = b + 1, b + 2
                if s == 2 and post:
                    dve.wait_ge(pv_done, 4 * b)
                    dve.wait_ge(r_ready, b)
                    v.tensor_tensor(ctxT[:, :, :], halves(context), halves(rbc), ALU.mult).then_inc(ctx_ready, 1)
                if s == 0 and layer0:
                    dve.wait_ge(x_loaded, 32 * n2 + 32)
                    apply(n2, 0, xf[:, :], mean1[:, bass.ds(n2, 1)], rstd1[:, bass.ds(n2, 1)])
                if s == 4 and layer0:
                    c = v_ln2a.start(n2)
                    dve.wait_ge(mid_ready, 2 * n2 + 2)
                    c.link(dve, v.bn_stats(mst[:, :], mid[:, :]))
                    hold(dve)
                    c.link(dve, v.bn_aggr(ln2["ba"][:, 0, :], mst[:, :]))
                    v.tensor_copy(mag[:, 0:1], ln2["ba"][:, 0, 0:1])
                    v.scalar_tensor_tensor(out=mag[:, 1:2], in0=ln2["ba"][:, 0, 0:1], scalar=ln2["ba"][:, 0, 0:1],
                                           in1=ln2["ba"][:, 0, 1:2], op0=ALU.mult, op1=ALU.add)\
                     .then_inc(mst_ready, 1)
                if s == 5 and layer0:
                    c = v_ln2b.start(n2)
                    dve.wait_ge(mst_done, n2 + 1)
                    c.link(dve, v.tensor_copy(mst2[:, :], M2[:, 0:2]))
                    c.link(dve, v.scalar_tensor_tensor(out=ln2["a"][:, :], in0=mst2[:, 0:1], scalar=mst2[:, 0:1],
                                                       in1=mst2[:, 1:2], op0=ALU.mult, op1=ALU.subtract))
                    c.link(dve, v.tensor_scalar(ln2["v"][:, :], ln2["a"][:, :], -1.0, EPS, ALU.mult, ALU.add))
                    seed(n2, c, ln2, seed2)
                if s in (10, 11, 12, 13) and post:
                    j = s - 10
                    dve.wait_ge(uth_ready, 4 * b - 4 + j + 1)
                    if j == 0:
                        need(dve, ff2_done, b - 1)
                    v.scalar_tensor_tensor(out=fT[:, 2 * j:2 * j + 2, :], in0=uth[:, 2 * j:2 * j + 2, :],
                                           scalar=1.0, in1=uT[:, 2 * j:2 * j + 2, :], op0=ALU.add,
                                           op1=ALU.mult).then_inc(f_ready, 1)
                if s == 15 and layer0:
                    dve.wait_ge(rs3, n2 + 1)
                    need(dve, nt_done, n2)
                    token_norm(xn, x1, ln3).then_inc(xn_ready, 1)
                if s == 15 and post:
                    dve.wait_ge(ff2_done, b)
                    dve.wait_ge(x2b_ready, b)
                    need(dve, out_stored, 16 * (b - 1))
                    v.tensor_tensor(outt[:, :], M1[:, :], x2b[:, :], ALU.add).then_inc(out_ready, 1)

            def turn(b, att, proj, layer0, post):
                for s in range(16):
                    if att:
                        softmax_max(b, s)
                    before(b, s, att, proj, layer0, post)
                    if (att if s >= LAG else post) and (s - LAG) % 16 not in ACT_MOVES:
                        probs_out(b - (s < LAG), (s - LAG) % 16)
                    after(b, s, att, proj, layer0, post)

            turns_of_the_loop(dve, turn)


def kernel(**inputs):
    import numpy as np
    import concourse.bacc as bacc
    from concourse.bass_utils import run_bass_kernel_spmd as run

    a = {k: np.asarray(x) for k, x in inputs.items()}

    def columns(x):
        return x.reshape(-1, P).T

    def rows_of(x):
        return x.reshape(-1, P, x.shape[1]).transpose(1, 0, 2).reshape(P, -1)

    half0, half1 = E // 2, D // 2
    f0 = np.exp(np.arange(half0, dtype=np.float32) * np.float32(-np.log(10000.0) / (half0 - 1)))
    f1 = np.exp(np.arange(half1, dtype=np.float32) * np.float32(-np.log(10000.0) / (half1 - 1)))
    consts = np.zeros((P, NCST), np.float32)
    consts[:, C_F0] = np.concatenate([f0, f0])
    consts[half0:, C_T0] = 0.25
    consts[half0:, C_O0] = TURN / 4
    consts[:, C_F1] = f1

    x = a["x"]
    order = [head_at(n)[0] for n in range(H)]
    fside = a["fside_Bx16xSxS_0"][:, order].reshape(B, GROUPS, GH, NC, P, S).transpose(0, 1, 4, 2, 3, 5)
    l0, l1 = "L0_cond_", "L1_cond_"
    arrays = {
        "x_tok": x.reshape(B, NC, P, D).transpose(0, 2, 1, 3).reshape(B, P, NC * D),
        "x_feat": x.transpose(0, 2, 1).reshape(B, NC, P, S).transpose(0, 2, 1, 3).reshape(B, P, NC * S),
        "cond_t": a["condB_t"],
        "step_t": a["itok_B_34_63"],
        "fside": fside.reshape(B, GROUPS, P, GH, NC * S),
        "mask": a["mask_Bx1xSxS_bk0"].reshape(B, NC, P, S).transpose(0, 2, 1, 3).reshape(B, P, NC * S),
        "gbT": np.stack([rows_of(a[l0 + n].T) for n in ("gamma", "beta")], 1),
        "wmain": np.concatenate([rows_of(a[n]) for n in (
            l0 + "W_in", l0 + "W_out", l1 + "Wq", l1 + "Wk", l1 + "Wv", l1 + "Wo", l1 + "W1", l1 + "W2")], 1),
        "wcond": np.concatenate([rows_of(a[n]) for n in (
            l0 + "W1", l0 + "W2", l0 + "Wsc", l0 + "Wsh", l1 + "W_ada")], 1),
        "vecs": np.concatenate([columns(a[n]) for n in (
            l0 + "b1", l0 + "b2", l0 + "bsc", l0 + "bsh", l0 + "b_in", l1 + "b_ada", l1 + "bq", l1 + "bk",
            l1 + "bv", l1 + "bo", l1 + "b1", l1 + "g2", l1 + "beta2")], 1),
        "consts": consts,
        "rows": np.stack([a[l0 + "b_out"], a[l1 + "b2"]]),
    }
    nc = bacc.Bacc("TRN2", target_bir_lowering=False, num_devices=1)
    args, fed = [], {}
    for name, value in arrays.items():
        value = np.ascontiguousarray(value)
        fed[f"in_{name}"] = value
        args.append(nc.dram_tensor(f"in_{name}", value.shape, mybir.dt.from_np(value.dtype),
                                   kind="ExternalInput").ap())
    out = nc.dram_tensor("out", (B, P, NC * D), F32, kind="ExternalOutput").ap()
    build(nc, *args, out)
    got = run(nc, [fed], core_ids=[0]).results[0]["out"]
    return np.ascontiguousarray(got.reshape(B, P, NC, D).transpose(0, 2, 1, 3).reshape(B, S, D))
```

```python
from contextlib import ExitStack

import concourse.bass as bass
from concourse import mybir

F32 = mybir.dt.float32
F32R = mybir.dt.float32r
I32 = mybir.dt.int32
U8 = mybir.dt.uint8
ALU = mybir.AluOpType
ACT = mybir.ActivationFunctionType

P = 128
B, S, D = 8, 256, 256
H, DH = 16, 16
E = 128
HID = 4 * E
FF = 1024
NC = D // P
NF = FF // P
NH = HID // P
GROUPS, GH = 4, 4
EPS = 1e-5
MASKED = -1e30
HUGE = 3e38
MAGIC = 1.5 * 2 ** 23
TURN = 6.283185307179586
TURN1 = 6.28125
TURN2 = 2029 / 2 ** 20
TURN3 = TURN - TURN1 - TURN2
ARC = 3.1415925
SEED = 1597463007.0

COLS = {}
for _name, _n in (("b1", NH), ("b2", NH), ("bsc", NC), ("bsh", NC), ("b_in", NC), ("ada", 2 * NC),
                  ("bq", NC), ("bk", NC), ("bv", NC), ("bo", NC), ("ff1", NF), ("g2", NC), ("beta2", NC)):
    COLS[_name] = (sum(n for _, n in COLS.values()), _n)
NCOL = sum(n for _, n in COLS.values())
C_F0, C_T0, C_O0, C_F1, NCST = range(5)
WAT = {}
for _name, _k, _n in (("in", NC, D), ("out", NC, D), ("q", NC, D), ("k", NC, D), ("v", NC, D),
                      ("o", NC, D), ("ff1", NC, FF), ("ff2", NF, D)):
    WAT[_name] = (sum(k * n for _, k, n in WAT.values()), _k, _n)
NW = sum(k * n for _, k, n in WAT.values())
W_L0 = WAT["q"][0]
CAT = {}
for _name, _k, _n in (("w1", 1, HID), ("w2", NH, HID), ("wsc", NH, D), ("wsh", NH, D), ("wada", NC, 2 * D)):
    CAT[_name] = (sum(k * n for _, k, n in CAT.values()), _k, _n)
NCW = sum(k * n for _, k, n in CAT.values())
R_OUT, R_FF2, NROW = range(3)
W_SC = CAT["wsc"][0]
HI, LO = range(2)
STACK = ((HI, LO, HI), (HI, HI, LO))
KROWS = 3 * DH
ACT_MOVES = (1, 2, 3, 4, 11, 12)
FF2_AT = {13: ((0, range(0, 4)),), 14: ((0, range(4, 8)),), 15: ((1, range(0, 4)),)}
FF2_LAST = (1, range(4, 8))
LAG = 2


def moved(b, n):
    if isinstance(n, int) and n < 0:
        b, n = b - 1, n + 16
    by_act = n in ACT_MOVES
    each = len(ACT_MOVES) if by_act else 16 - len(ACT_MOVES)
    return by_act, b * each + sum((m in ACT_MOVES) == by_act for m in range(n + 1))


def head_at(n):
    g, band = divmod(n, GH)
    chunk, odd = divmod(g, 2)
    return 8 * chunk + 2 * band + odd, band, chunk, odd


def hold(engine):
    engine.nop(nofuse=True)


class Chain:

    def __init__(self, sem, per, held=False):
        self.sem, self.per, self.held = sem, per, held

    def start(self, b, at=0):
        self.b, self.at = b, at
        return self

    def link(self, engine, instruction):
        self.at += 1
        assert self.at <= self.per
        instruction.then_inc(self.sem, 1)
        engine.wait_ge(self.sem, self.b * self.per + self.at)
        if self.held:
            hold(engine)


def need(engine, sem, value):
    if not isinstance(value, int) or value > 0:
        engine.wait_ge(sem, value)


def build(nc, x_tok, x_feat, cond_t, step_t, fside, mask, gbT, wmain, wcond, vecs, consts, rows, out):
    with ExitStack() as ctx:
        def sb(name, shape, dt=F32):
            return ctx.enter_context(nc.sbuf_tensor(name, shape, dt))

        def psum(name):
            return ctx.enter_context(nc.psum_tensor(name, [P, 512], F32))

        def sem(name):
            return ctx.enter_context(nc.semaphore(name))

        w = sb("w", [P, NW])
        gb = sb("gb", [P, 2, NC * S])
        vec = sb("vec", [P, NCOL])
        cst = sb("cst", [P, NCST])
        brow = sb("brow", [P, NROW, D])
        ident = sb("ident", [P, P])
        mean_of = sb("mean_of", [P, P])
        tb = sb("tb", [P, B])
        tsi = sb("tsi", [P, B], I32)
        bns = sb("bns", [P, B, 6])
        bna = sb("bna", [P, B, 2])
        st1 = sb("st1", [P, 2, B])
        mean1 = sb("mean1", [P, B])
        rstd1 = sb("rstd1", [P, B])
        var1 = sb("var1", [P, B])
        angle = sb("angle", [P, 3, B])
        turns = sb("turns", [P, 3, B])
        emb = sb("emb", [P, 3, B])
        embh = sb("embh", [P, 3, B])
        h1 = sb("h1", [P, NH, B])
        h1t = sb("h1t", [P, NH, B])
        h2 = sb("h2", [P, NH, B])
        half_sc = sb("half_sc", [P, NC, B])
        half_sh = sb("half_sh", [P, NC, B])
        ada = sb("ada", [P, 2 * NC, B])
        bq4 = sb("bq4", [P, NC])
        bov = sb("bov", [P, NC])

        xt = sb("xt", [P, NC * D])
        xf = sb("xf", [P, NC * S])
        xb = sb("xb", [P, NC * D])
        lna = sb("lna", [P, NC * S])
        lny = sb("lny", [P, NC * S])
        qk_part = sb("qk_part", [P, 2, 2, NC * S], F32R)
        lnt = sb("lnt", [P, NC * S])
        hin = sb("hin", [P, NC * S])
        mid = sb("mid", [P, NC * S])
        mst = sb("mst", [P, 6])
        mag = sb("mag", [P, 2])
        mst2 = sb("mst2", [P, 2])
        x1 = sb("x1", [P, NC, D])
        xn = sb("xn", [P, NC * D])
        xaT = sb("xaT", [P, NC, S])
        xres = sb("xres", [P, NC, S])
        stack = sb("stack", [64, 2, H, S], F32R)
        parts = nc.dram_tensor("parts", [2, 2, P, NC * S], F32R).ap()
        vpad = sb("vpad", [P, NC, H, 2 * DH])
        m8 = sb("m8", [P, NC * S], U8)
        maskneg = sb("maskneg", [P, NC * S])
        bias = sb("bias", [P, GROUPS, GH, NC * S])
        sneg = sb("sneg", [P, 2, NC, S])
        negmax = sb("negmax", [P, NC, H])
        prob = sb("prob", [P, 2, NC, S])
        rsum = sb("rsum", [P, NC, H])
        rinv = sb("rinv", [P, NC, H])
        rinvx = sb("rinvx", [P, NC, H, DH])
        room2 = sb("room2", [P, 2 * GH * NC * S + NF * S])
        probT = room2[:, 0:2 * GH * NC * S].rearrange("p (n s) -> p n s", n=2 * GH)
        fT = room2[:, 2 * GH * NC * S:].rearrange("p (m s) -> p m s", m=NF)
        cw = room2
        rbc = sb("rbc", [P, NC * S])
        ctxT = sb("ctxT", [P, NC, S])
        x2 = sb("x2", [P, NC, D])
        x2b = sb("x2b", [P, NC * D])
        x2n = sb("x2n", [P, NC * D])
        hT = sb("hT", [P, NC, S])
        room = sb("room", [P, B, NC * S])
        uT = room[:, 0:NF // 2, :].rearrange("p a (m n) -> p (a m) n", m=2)
        uth = room[:, NF // 2:NF, :].rearrange("p a (m n) -> p (a m) n", m=2)
        xall = room
        outt = sb("outt", [P, NC * D])

        row = outt[0:B, :]

        def newton_buffers(name, n):
            return {k: sb(f"{name}_{k}", [P, n], I32 if k in ("h", "s") else F32) for k in "vhsnar"} | {
                "bs": sb(f"{name}_bs", [P, NC, 6]), "ba": sb(f"{name}_ba", [P, NC, 2])}

        ln2, ln3, ln4 = (newton_buffers(f"ln{i}", n) for i, n in ((2, 1), (3, NC), (4, NC)))

        score = [psum("score0"), psum("score1")]
        trans = [psum("trans0"), psum("trans1")]
        context = psum("context")
        M0, M1, M2 = psum("M0"), psum("M1"), psum("M2")

        def W(name):
            at, k, n = WAT[name]
            return w[:, at:at + k * n].rearrange("p (k n) -> p k n", k=k)

        def CW(name):
            at, k, n = CAT[name]
            return cw[:, at:at + k * n].rearrange("p (k n) -> p k n", k=k)

        def col(name, i=0, n=1):
            return vec[:, COLS[name][0] + i:COLS[name][0] + i + n]

        def halves(t):
            return t[:, :].rearrange("p (c n) -> p c n", c=2)

        small_loaded, cond1_loaded, cond2_loaded, cond_loaded, xall_loaded, layer0_loaded, weights_loaded = map(
            sem, ("small_loaded", "cond1_loaded", "cond2_loaded", "cond_loaded", "xall_loaded", "layer0_loaded", "weights_loaded"))
        scaled = sem("scaled")
        x_loaded, mask_loaded = sem("x_loaded"), sem("mask_loaded")
        bias_loaded = [sem(f"bias_loaded{g}") for g in range(GROUPS)]
        out_stored = sem("out_stored")
        ident_ready, zeros_ready = sem("ident_ready"), sem("zeros_ready")
        st1_ready, st1_done, var1_ready, std1_ready, angle_ready, emb_ready, embt_ready, embs_ready = map(
            sem, ("st1_ready", "st1_done", "var1_ready", "std1_ready", "angle_ready", "emb_ready",
                  "embt_ready", "embs_ready"))
        w1_done, h1_ready, h1t_ready, h1s_ready, w2_done, h2_ready, wsc_done, wada_done, bov_done, setup_ready, bov_ready, row_ready, w2t_done, wsct_done = map(
            sem, ("w1_done", "h1_ready", "h1t_ready", "h1s_ready", "w2_done", "h2_ready", "wsc_done",
                  "wada_done", "bov_done", "setup_ready", "bov_ready", "row_ready", "w2t_done", "wsct_done"))
        v_setup, v_late = Chain(sem("v_setup"), 64), Chain(sem("v_late"), 1)
        bias_ready, qk_done, smax_done, exp_done, tr_done, pt_dve, pt_act = map(
            sem, ("bias_ready", "qk_done", "smax_done", "exp_done", "tr_done", "pt_dve", "pt_act"))
        pv_done = sem("pv_done")
        xb_ready, y_ready, tanh_ready, hin_ready, win_done, mid_ready = map(
            sem, ("xb_ready", "y_ready", "tanh_ready", "hin_ready", "win_done", "mid_ready"))
        mst_ready, mst_done, seed2, rs2, wout_done, x1_ready = map(
            sem, ("mst_ready", "mst_done", "seed2", "rs2", "wout_done", "x1_ready"))
        seed3, rs3, xn_ready, nt_done, xaT_ready, xres_ready = map(
            sem, ("seed3", "rs3", "xn_ready", "nt_done", "xaT_ready", "xres_ready"))
        q_done, k_done, v_done, hi_ready, lo_ready, parts_stored, stack_loaded0, stack_loaded1, v_ready = map(
            sem, ("q_done", "k_done", "v_done", "hi_ready", "lo_ready", "parts_stored",
                  "stack_loaded0", "stack_loaded1", "v_ready"))
        stack_loaded = (stack_loaded0, stack_loaded1)
        mask_ready, mask_read = sem("mask_ready"), sem("mask_read")
        rinv_ready, rinvx_ready, r_done, r_ready, ctx_ready, wo_done, x2_ready = map(
            sem, ("rinv_ready", "rinvx_ready", "r_done", "r_ready", "ctx_ready", "wo_done", "x2_ready"))
        seed4, rs4, x2b_ready, x2n_ready, n2t_done, hT_ready = map(
            sem, ("seed4", "rs4", "x2b_ready", "x2n_ready", "n2t_done", "hT_ready"))
        ff1_done, u_ready, uth_ready, f_ready, ff2_done, out_ready = map(
            sem, ("ff1_done", "u_ready", "uth_ready", "f_ready", "ff2_done", "out_ready"))
        v_apply, v_ln2a, v_ln2b, v_ln3, v_ln4 = (
            Chain(sem(n), k) for n, k in (("v_apply", 4), ("v_ln2a", 2), ("v_ln2b", 4), ("v_ln3", 4), ("v_ln4", 4)))
        v_newton = Chain(sem("v_newton"), 6)
        p_rs2, p_rs3, p_rs4 = (Chain(sem(n), 6, True) for n in ("p_rs2", "p_rs3", "p_rs4"))

        def mm(pe, o, lhsT, rhs, start=True, stop=True):
            return nc.tensor.matmul(o, lhsT, rhs, start=start, stop=stop)

        def newton(engine, ops, c, t, n, done):
            c.link(engine, ops.tensor_scalar(t["n"][:, :], t["v"][:, :], -0.5, None, ALU.mult))
            r = t["s"][:, :].bitcast(F32)
            for i in range(3):
                for j in range(n):
                    a = ops.tensor_scalar(t["a"][:, j:j + 1], r[:, j:j + 1], r[:, j:j + 1],
                                          t["n"][:, j:j + 1], ALU.mult, ALU.mult)
                c.link(engine, a)
                for j in range(n):
                    a = ops.tensor_scalar(t["r"][:, j:j + 1], t["a"][:, j:j + 1], 1.5,
                                          r[:, j:j + 1], ALU.add, ALU.mult)
                if i < 2:
                    c.link(engine, a)
                r = t["r"][:, :]
            a.then_inc(done, 1)

        block = ctx.enter_context(nc.Block())

        def turns_of_the_loop(engine, turn):
            turn(-2, False, False, True, False, False)
            turn(-1, False, True, True, False, False)
            turn(0, True, True, True, False, False)
            turn(1, True, True, True, True, False)
            with engine.Fori(2, B - 2) as b:
                turn(b, True, True, True, True, True)
            turn(B - 2, True, True, False, True, True)
            turn(B - 1, True, False, False, True, True)
            turn(B, False, False, False, True, True)

        @block.sync
        def _(sp):
            sp.dma_start(vec[:, :], vecs).then_inc(small_loaded, 16)
            sp.dma_start(cst[:, :], consts).then_inc(small_loaded, 16)
            sp.dma_start(tb[:, :], cond_t.partition_broadcast(P)).then_inc(small_loaded, 16)
            sp.dma_start(tsi[:, :], step_t.partition_broadcast(P)).then_inc(small_loaded, 16)
            sp.dma_start(cw[:, 0:HID], wcond[:, 0:HID]).then_inc(cond1_loaded, 16)
            sp.dma_start(cw[:, HID:W_SC], wcond[:, HID:W_SC]).then_inc(cond2_loaded, 16)
            sp.dma_start(xall[:, :, :], x_feat.rearrange("b p n -> p b n")).then_inc(xall_loaded, 16)
            sp.dma_start(cw[:, W_SC:NCW], wcond[:, W_SC:NCW]).then_inc(cond_loaded, 16)
            sp.dma_start(gb[:, :, :], gbT).then_inc(layer0_loaded, 16)
            sp.dma_start(w[:, 0:W_L0], wmain[:, 0:W_L0]).then_inc(layer0_loaded, 16)

            def load_x(b):
                need(sp, xb_ready, b)
                need(sp, v_apply.sem, 4 * b - 3)
                hold(sp)
                sp.dma_start(xf[:, :], x_feat[b, :, :]).then_inc(x_loaded, 16)
                sp.dma_start(xt[:, :], x_tok[b, :, :]).then_inc(x_loaded, 16)

            def load_bias(b, g):
                need(sp, smax_done, 16 * (b - 1) + GH * (g + 1))
                hold(sp)
                sp.dma_start(bias[:, g, :, :], fside[b, g, :, :]).then_inc(bias_loaded[g], 16)

            def store(b):
                sp.wait_ge(out_ready, b + 1)
                hold(sp)
                sp.dma_start(out[b, :, :], outt[:, :]).then_inc(out_stored, 16)

            def restack(b, c):
                need(sp, qk_done, 16 * (b - 1) + 8 * (c + 1))
                hold(sp)
                for i in range(2):
                    for j, part in enumerate(STACK[i]):
                        sp.dma_start(
                            stack[DH * j:DH * (j + 1), i, 8 * c:8 * c + 8, :].bitcast(F32),
                            parts[i, part, :, c * S:(c + 1) * S].rearrange("(h d) s -> d h s", d=DH).bitcast(F32))\
                          .then_inc(stack_loaded[c], 16)

            def turn(b, att, proj, layer0, post, finish):
                if finish:
                    store(b - 2)
                if proj:
                    need(sp, mask_ready, b + 1)
                    hold(sp)
                    sp.dma_start(m8[:, :], mask[b + 1, :, :]).then_inc(mask_loaded, 16)
                    load_bias(b + 1, 0)
                    load_bias(b + 1, 1)
                    for c in range(2):
                        need(sp, stack_loaded[c], 96 * b + 96)
                    for i in range(2):
                        sp.wait_ge(hi_ready, 2 * b + 3 + i)
                        sp.wait_ge(lo_ready, 2 * b + 3 + i)
                        hold(sp)
                        sp.dma_start(parts[i, :, :, :].rearrange("a p n -> p a n").bitcast(F32),
                                     qk_part[:, i, :, :].bitcast(F32)).then_inc(parts_stored, 16)
                    sp.wait_ge(parts_stored, 32 * b + 64)
                    restack(b + 1, 0)
                    load_bias(b + 1, 2)
                if layer0 and not (isinstance(b, int) and b == B - 3):
                    load_x(b + 3)
                if proj:
                    load_bias(b + 1, 3)
                    restack(b + 1, 1)
                if post and not att:
                    store(b - 1)

            load_x(0)
            sp.dma_start(brow[:, :, :], rows.partition_broadcast(P)).then_inc(weights_loaded, 16)
            sp.dma_start(w[:, W_L0:NW], wmain[:, W_L0:NW]).then_inc(weights_loaded, 16)
            turn(-2, False, False, True, False, False)
            turn(-1, False, True, True, False, False)
            turn(0, True, True, True, False, False)
            turn(1, True, True, True, True, False)
            with sp.Fori(2, B - 3) as b:
                turn(b, True, True, True, True, True)
            turn(B - 3, True, True, True, True, True)
            turn(B - 2, True, True, False, True, True)
            turn(B - 1, True, False, False, True, True)
            turn(B, False, False, False, True, True)
            sp.wait_ge(out_stored, 16 * B)

        @block.gpsimd
        def _(pool):
            nc.gpsimd.memset(ident[:, :], 0.0).then_inc(zeros_ready, 1)
            nc.gpsimd.memset(mean_of[:, :], 1.0 / P).then_inc(ident_ready, 1)
            nc.gpsimd.memset(vpad[:, :, :, :], 0.0).then_inc(ident_ready, 1)
            pool.wait_ge(zeros_ready, 1)
            nc.gpsimd.affine_select(out=ident[:, :], in_=ident[:, :], compare_op=ALU.not_equal, fill=1.0,
                                    base=0, pattern=[[-1, P]], channel_multiplier=1).then_inc(ident_ready, 1)

            def rsqrt(b, first, chain, t, n, seeded, done):
                pool.wait_ge(seeded, b + 1)
                hold(pool)
                newton(pool, nc.gpsimd, chain.start(b - first), t, n, done)

            def mask_heads(b, g, heads):
                if 0 in heads:
                    pool.wait_ge(bias_loaded[g], 16 * b + 16)
                for i in heads:
                    nc.gpsimd.tensor_tensor(bias[:, g, i, :], bias[:, g, i, :], maskneg[:, :],
                                            ALU.add).then_inc(bias_ready, 1)

            pool.wait_ge(weights_loaded, 32)
            nc.gpsimd.tensor_scalar(W("q"), W("q"), DH ** -0.5, None, ALU.mult).then_inc(scaled, 1)

            def mask_out(b):
                pool.wait_ge(mask_loaded, 16 * b + 16)
                need(pool, bias_ready, 16 * b)
                hold(pool)
                nc.gpsimd.tensor_scalar(maskneg[:, :], m8[:, :], MASKED, None, ALU.mult).then_inc(mask_ready, 1)
                pool.wait_ge(mask_ready, b + 1)

            def turn(b, att, proj, layer0, post, finish):
                n1, n2 = b + 1, b + 2
                if att:
                    mask_heads(b, 2, range(GH))
                if proj and att:
                    rsqrt(n1, 1, p_rs3, ln3, NC, seed3, rs3)
                if post and att:
                    rsqrt(b - 1, 0, p_rs4, ln4, NC, seed4, rs4)
                if att:
                    mask_heads(b, 3, range(GH))
                if post:
                    pool.wait_ge(x2_ready, b)
                    need(pool, out_ready, b - 1)
                    nc.gpsimd.tensor_tensor(halves(x2b), x2[:, :, :],
                                            brow[:, R_FF2, :].unsqueeze(1).to_broadcast([P, NC, D]),
                                            ALU.add).then_inc(x2b_ready, 1)
                if layer0:
                    need(pool, x1_ready, n2)
                    pool.wait_ge(x_loaded, 32 * n2 + 32)
                    nc.gpsimd.tensor_tensor(halves(xb), halves(xt),
                                            brow[:, R_OUT, :].unsqueeze(1).to_broadcast([P, NC, D]),
                                            ALU.add).then_inc(xb_ready, 1)
                if proj:
                    mask_out(n1)
                    for g in (0, 1):
                        mask_heads(n1, g, range(GH))
                if proj and not att:
                    nc.gpsimd.tensor_scalar(W("ff2"), W("ff2"), 0.5, None, ALU.mult).then_inc(scaled, 1)
                if layer0 and att:
                    rsqrt(n2, 2, p_rs2, ln2, 1, seed2, rs2)

            turns_of_the_loop(pool, turn)

        @block.tensor
        def _(pe):
            pe.wait_ge(ident_ready, 3)
            pe.wait_ge(cond1_loaded, 16)
            pe.wait_ge(emb_ready, 1)
            for m in range(NH):
                last = mm(pe, M0[:, m * B:(m + 1) * B], CW("w1")[:, 0, m * P:(m + 1) * P], emb[:, 0, :])
            last.then_inc(w1_done, 1)
            pe.wait_ge(cond2_loaded, 16)
            pe.wait_ge(h1s_ready, 1)
            for k in range(NH):
                last = mm(pe, M1[0:B, :], h1[:, k, :], CW("w2")[:, k, :], k == 0, k == NH - 1)
            last.then_inc(w2_done, 1)

            def row_turned(bank, done):
                for m in range(NH):
                    last = nc.tensor.transpose(bank[:, m * B:(m + 1) * B], row[:, m * P:(m + 1) * P],
                                               ident[0:B, 0:B])
                last.then_inc(done, 1)

            pe.wait_ge(row_ready, 1)
            row_turned(M1, w2t_done)
            pe.wait_ge(h2_ready, 1)
            pe.wait_ge(cond_loaded, 16)
            for j, name in enumerate(("wsc", "wsh")):
                for k in range(NH):
                    last = mm(pe, M0[0:B, j * D:(j + 1) * D], h2[:, k, :], CW(name)[:, k, :], k == 0, k == NH - 1)
            last.then_inc(wsc_done, 1)
            pe.wait_ge(st1_ready, 1)
            mm(pe, M2[:, 0:2 * B], mean_of[:, :], st1[:, :, :]).then_inc(st1_done, 1)
            pe.wait_ge(row_ready, 2)
            row_turned(M0, wsct_done)
            pe.wait_ge(embs_ready, 1)
            for m in range(2 * NC):
                for k in range(NC):
                    last = mm(pe, M1[:, m * B:(m + 1) * B], CW("wada")[:, k, m * P:(m + 1) * P],
                              embh[:, 1 + k, :], k == 0, k == NC - 1)
            last.then_inc(wada_done, 1)
            pe.wait_ge(layer0_loaded, 32)

            def scores(b, n):
                h, band, c, odd = head_at(n)
                if n % 8 == 0:
                    pe.wait_ge(stack_loaded[c], 96 * b + 96)
                need(pe, smax_done, 16 * b + n - 1)
                for t in range(NC):
                    last = mm(pe, score[n % 2][:, t * S:(t + 1) * S], stack[0:KROWS, 0, h, t * P:(t + 1) * P],
                              stack[0:KROWS, 1, h, :])
                last.then_inc(qk_done, 1)

            def turned_out(b, n):
                by_act, count = moved(b, n)
                need(pe, pt_act if by_act else pt_dve, count)

            def turn_probs(b, n):
                pe.wait_ge(exp_done, 16 * b + n + 1)
                turned_out(b, n - 2)
                for k in range(NC):
                    for t in range(NC):
                        last = nc.tensor.transpose(trans[n % 2][:, k * S + t * P:k * S + (t + 1) * P],
                                                   prob[:, n % 2, t, k * P:(k + 1) * P], ident[:, :])
                last.then_inc(tr_done, 1)

            def values(b, g):
                for n in {moved(0, n)[0]: n for n in range(GH * g, GH * (g + 1))}.values():
                    turned_out(b, n)
                pe.wait_ge(v_ready, b + 1)
                if g == 0:
                    need(pe, ctx_ready, b)
                for k in range(NC):
                    for i in range(GH):
                        h, band, c, odd = head_at(GH * g + i)
                        last = mm(pe, context[32 * band:32 * band + 32, c * S:(c + 1) * S], vpad[:, k, h, :],
                                  probT[:, (g % 2) * GH + i, k * S:(k + 1) * S],
                                  k == 0 and odd == 0, k == NC - 1 and odd == 1)
                last.then_inc(pv_done, 1)

            def features_out(bank, name, src):
                for m in range(NC):
                    for k in range(NC):
                        last = mm(pe, bank[:, m * S:(m + 1) * S], W(name)[:, k, m * P:(m + 1) * P], src[:, k, :],
                                  k == 0, k == NC - 1)
                return last

            def tokens_out(bank, name, src, add=None):
                for t in range(NC):
                    for k in range(NC):
                        last = mm(pe, bank[:, t * D:(t + 1) * D], src[:, k, t * P:(t + 1) * P], W(name)[:, k, :],
                                  k == 0, k == NC - 1)
                    if add is not None:
                        for c in range(NC):
                            last = nc.tensor.matmul(bank[:, t * D + c * P:t * D + (c + 1) * P],
                                                    add[:, c, t * P:(t + 1) * P], ident[:, :],
                                                    start=False, stop=True, is_transpose=True,
                                                    skip_group_check=True)
                return last

            def turned(bank, src):
                for c in range(NC):
                    for t in range(NC):
                        last = nc.tensor.transpose(bank[:, c * S + t * P:c * S + (t + 1) * P],
                                                   src[:, t * D + c * P:t * D + (c + 1) * P], ident[:, :])
                return last

            def ff1(b, j, bank):
                pe.wait_ge(hT_ready, 2 * b)
                for i in range(2):
                    m = 2 * j + i
                    for k in range(NC):
                        last = mm(pe, bank[:, i * S:(i + 1) * S], W("ff1")[:, k, m * P:(m + 1) * P], hT[:, k, :],
                                  k == 0, k == NC - 1)
                last.then_inc(ff1_done, 1)

            def ff2(b, t, ks):
                for k in ks:
                    last = mm(pe, M1[:, t * D:(t + 1) * D], fT[:, k, t * P:(t + 1) * P], W("ff2")[:, k, :],
                              k == 0, k == NF - 1)
                return last

            def bov_product():
                pe.wait_ge(weights_loaded, 32)
                pe.wait_ge(setup_ready, 1)
                pe.wait_ge(small_loaded, 64)
                for m in range(NC):
                    for k in range(NC):
                        last = mm(pe, M1[:, m:m + 1], W("o")[:, k, m * P:(m + 1) * P],
                                  col("bv", k), k == 0, k == NC - 1)
                last.then_inc(bov_done, 1)

            def filler(b, s, att, proj, layer0, post, finish):
                n1, n2 = b + 1, b + 2
                if s == 0 and proj and not att:
                    bov_product()
                if s == 0 and finish:
                    ff2(b - 2, *FF2_LAST).then_inc(ff2_done, 1)
                if s == 1 and post:
                    if att:
                        pe.wait_ge(lo_ready, 2 * b + 1)
                    need(pe, u_ready, 8 * b - 8)
                    pe.wait_ge(rinvx_ready, b)
                    for c in range(NC):
                        for t in range(NC):
                            last = nc.tensor.transpose(
                                M2[:, c * S + t * P:c * S + (t + 1) * P],
                                rinvx[:, t, 8 * c:8 * c + 8, :].rearrange("p h d -> p (h d)"), ident[:, :])
                    last.then_inc(r_done, 1)
                if s == 3 and proj:
                    pe.wait_ge(hin_ready, 2 * n1 + 2)
                    pe.wait_ge(v_ln2b.sem, 4 * n1 + 1)
                    tokens_out(M0, "out", halves(hin)).then_inc(wout_done, 1)
                if s == 4 and post:
                    pe.wait_ge(ctx_ready, b)
                    need(pe, out_ready, b - 1)
                    pe.wait_ge(xres_ready, 2 * b)
                    tokens_out(M1, "o", ctxT, xres).then_inc(wo_done, 1)
                if s == 5 and att:
                    pe.wait_ge(xaT_ready, 2 * b + 2)
                    if proj:
                        pe.wait_ge(x1_ready, n1 + 1)
                    else:
                        pe.wait_ge(lo_ready, 2 * b + 2)
                    tokens_out(M0, "v", xaT).then_inc(v_done, 1)
                if s == 7 and proj:
                    pe.wait_ge(xn_ready, n1 + 1)
                    if att:
                        pe.wait_ge(v_ready, b + 1)
                    turned(M0, xn).then_inc(nt_done, 1)
                if s == 8 and proj:
                    pe.wait_ge(xaT_ready, 2 * n1 + 2)
                    pe.wait_ge(scaled, 1)
                    if post:
                        pe.wait_ge(r_ready, b)
                    else:
                        need(pe, lo_ready, 2 * n1)
                    features_out(M2, "q", xaT).then_inc(q_done, 1)
                if s == 8 and post:
                    pe.wait_ge(x2n_ready, b)
                    turned(M1, x2n).then_inc(n2t_done, 1)
                if s == 9 and proj:
                    features_out(M0, "k", xaT).then_inc(k_done, 1)
                if s in (9, 10, 11, 12) and post:
                    j = s - 9
                    if j == 1:
                        need(pe, lo_ready, 2 * n1 + 1 if proj else 0)
                        pe.wait_ge(r_ready, b)
                    if j >= 2:
                        pe.wait_ge(u_ready, 8 * b - 8 + 2 * (j - 1))
                    ff1(b, j, (M1, M2)[j % 2])
                if s == 11 and layer0:
                    pe.wait_ge(hin_ready, 2 * n2 + 1)
                    need(pe, lo_ready, 2 * n1 + 2 if proj else 0)
                    features_out(M0, "in", halves(hin)).then_inc(win_done, 1)
                if s == 12 and layer0:
                    pe.wait_ge(mst_ready, n2 + 1)
                    pe.wait_ge(mid_ready, 2 * n2 + 2)
                    mm(pe, M0[:, 0:2], mean_of[:, :], mag[:, :]).then_inc(mst_done, 1)
                for t, ks in FF2_AT.get(s, ()) if post else ():
                    pe.wait_ge(scaled, 2)
                    pe.wait_ge(f_ready, 4 * b - 4 + ks.stop // 2)
                    pe.wait_ge(u_ready, 8 * b - 2)
                    ff2(b, t, ks)
                if s == 15 and post and not att:
                    ff2(b, *FF2_LAST).then_inc(ff2_done, 1)

            def turn(b, att, proj, layer0, post, finish):
                for s in range(16):
                    if att:
                        scores(b, s)
                    if s < LAG:
                        if post:
                            turn_probs(b - 1, s - LAG + 16)
                    elif att:
                        turn_probs(b, s - LAG)
                    filler(b, s, att, proj, layer0, post, finish)
                    if s == LAG + 1:
                        if post:
                            values(b - 1, GROUPS - 1)
                    elif s % GH == LAG + 1 and att:
                        values(b, s // GH - 1)

            turns_of_the_loop(pe, turn)

        @block.scalar
        def _(act):
            act.wait_ge(angle_ready, 1)
            nc.scalar.activation(emb[:, :, :], angle[:, :, :], ACT.Sin).then_inc(emb_ready, 1)
            act.wait_ge(emb_ready, 1)
            nc.scalar.activation(embh[:, :, :], emb[:, :, :], ACT.Tanh, scale=0.5).then_inc(embt_ready, 1)
            act.wait_ge(h1_ready, 1)
            nc.scalar.activation(h1t[:, :, :], h1[:, :, :], ACT.Tanh, scale=0.5).then_inc(h1t_ready, 1)
            act.wait_ge(var1_ready, 1)
            nc.scalar.activation(rstd1[:, :], var1[:, :], ACT.Sqrt).then_inc(std1_ready, 1)

            def exps(b, n):
                h = head_at(n)[0]
                act.wait_ge(smax_done, 16 * b + n + 1)
                need(act, tr_done, 16 * b + n - 1)
                if n == 0:
                    need(act, rinv_ready, b)
                for t in range(NC):
                    last = nc.scalar.activation(prob[:, n % 2, t, :], sneg[:, n % 2, t, :], ACT.Exp,
                                                bias=negmax[:, t, h:h + 1], scale=-1.0,
                                                accum_out=rsum[:, t, h:h + 1])
                last.then_inc(exp_done, 1)

            def tanh_of(b, k):
                act.wait_ge(y_ready, 2 * b + 1 + k)
                need(act, hin_ready, 2 * b + k)
                nc.scalar.activation(lnt[:, :], lny[:, :], ACT.Tanh).then_inc(tanh_ready, 1)

            def filler(b, s, att, proj, layer0, post, finish):
                n1, n2 = b + 1, b + 2
                if s == 1 and post:
                    act.wait_ge(r_done, b)
                    need(act, ctx_ready, b - 1)
                    nc.scalar.activation(rbc[:, :], M2[:, :], ACT.Copy).then_inc(r_ready, 1)
                if s == 4 and post:
                    act.wait_ge(wo_done, b)
                    need(act, x2b_ready, b - 1)
                    nc.scalar.activation(x2[:, :, :], halves(M1), ACT.Copy).then_inc(x2_ready, 1)
                if s == 4 and att:
                    act.wait_ge(xaT_ready, 2 * b + 2)
                    act.wait_ge(bov_ready, 1)
                    need(act, wo_done, b)
                    for c in range(NC):
                        nc.scalar.activation(xres[:, c, :], xaT[:, c, :], ACT.Identity,
                                             bias=bov[:, c:c + 1]).then_inc(xres_ready, 1)
                if s == 5 and att:
                    act.wait_ge(v_done, b + 1)
                    need(act, pv_done, 4 * b)
                    for odd in range(2):
                        src = M0[:, :].rearrange("p (t h o d) -> p t h o d", t=NC, o=2, d=DH)
                        dst = vpad[:, :, :, odd * DH:(odd + 1) * DH].rearrange("p t (h o) d -> p t h o d", o=2)
                        last = nc.scalar.activation(dst[:, :, :, odd, :], src[:, :, :, odd, :], ACT.Copy)
                    last.then_inc(v_ready, 1)
                if s == 7 and proj:
                    if not att:
                        act.wait_ge(setup_ready, 1)
                    act.wait_ge(nt_done, n1 + 1)
                    if att:
                        act.wait_ge(v_done, b + 1)
                        act.wait_ge(xres_ready, 2 * b + 2)
                    for c in range(NC):
                        at = ada[:, NC + c, bass.ds(n1, 1)]
                        nc.scalar.activation(xaT[:, c, :], M0[:, c * S:(c + 1) * S], ACT.Identity,
                                             bias=at, scale=ada[:, c, bass.ds(n1, 1)]).then_inc(xaT_ready, 1)
                if s == 11 and layer0:
                    act.wait_ge(win_done, n2 + 1)
                    for m in range(NC):
                        nc.scalar.activation(mid[:, m * S:(m + 1) * S], M0[:, m * S:(m + 1) * S], ACT.Identity,
                                             bias=col("b_in", m)).then_inc(mid_ready, 1)
                if s in (8, 9) and proj:
                    i = s - 8
                    bank = (M2, M0)[i]
                    act.wait_ge((q_done, k_done)[i], n1 + 1)
                    need(act, parts_stored, 32 * n1)
                    need(act, lo_ready, 2 * n1)
                    for c in range(NC):
                        last = nc.scalar.activation(qk_part[:, i, HI, c * S:(c + 1) * S], bank[:, c * S:(c + 1) * S],
                                                    ACT.Identity, bias=bq4[:, c:c + 1] if i == 0 else col("bk", c))
                    last.then_inc(hi_ready, 1)
                if s in (10, 15) and layer0:
                    tanh_of(n2, int(s == 15))
                if s == 8 and post:
                    act.wait_ge(n2t_done, b)
                    for c in range(NC):
                        nc.scalar.activation(hT[:, c, :], M1[:, c * S:(c + 1) * S], ACT.Identity,
                                             bias=col("beta2", c), scale=col("g2", c)).then_inc(hT_ready, 1)
                if s in (9, 10, 11, 12) and post:
                    j = s - 9
                    act.wait_ge(ff1_done, 4 * b - 4 + j + 1)
                    bank = (M1, M2)[j % 2]
                    need(act, f_ready, 4 * (b - 1))
                    for i in range(2):
                        m = 2 * j + i
                        nc.scalar.activation(uT[:, m, :], bank[:, i * S:(i + 1) * S], ACT.Identity,
                                             bias=col("ff1", m)).then_inc(u_ready, 1)
                    act.wait_ge(u_ready, 8 * b - 8 + 2 * (j + 1))
                    nc.scalar.activation(uth[:, 2 * j:2 * j + 2, :], uT[:, 2 * j:2 * j + 2, :], ACT.Tanh,
                                         scale=0.5 * 1.702).then_inc(uth_ready, 1)

            def move(b, n):
                act.wait_ge(tr_done, 16 * b + n + 1)
                need(act, pv_done, 4 * b + n // GH - 1)
                nc.scalar.activation(probT[:, n % 8, :], trans[n % 2][:, :], ACT.Copy).then_inc(pt_act, 1)

            def turn(b, att, proj, layer0, post, finish):
                for s in range(16):
                    if att:
                        exps(b, s)
                    if (att if s >= LAG else post) and (s - LAG) % 16 in ACT_MOVES:
                        move(b - (s < LAG), (s - LAG) % 16)
                    filler(b, s, att, proj, layer0, post, finish)

            turns_of_the_loop(act, turn)

        @block.vector
        def _(dve):
            v = nc.vector
            c = v_setup.start(0)

            dve.wait_ge(small_loaded, 64)
            v.tensor_scalar(tb[:, :], tb[:, :], 5000.0, None, ALU.mult)
            c.link(dve, v.tensor_copy(angle[:, 2, :], tsi[:, :]))
            c.link(dve, v.tensor_scalar(angle[:, 2, :], angle[:, 2, :], 0.01, 4000.0, ALU.mult, ALU.mult))
            v.tensor_scalar(angle[:, 0, :], tb[:, :], cst[:, C_F0:C_F0 + 1], None, ALU.mult)
            v.tensor_scalar(angle[:, 1, :], angle[:, 2, :], cst[:, C_F1:C_F1 + 1], None, ALU.mult)
            c.link(dve, v.tensor_scalar(angle[:, 2, :], angle[:, 2, :], cst[:, C_F1:C_F1 + 1], None, ALU.mult))
            v.tensor_scalar(turns[:, 0, :], angle[:, 0, :], 1 / TURN, cst[:, C_T0:C_T0 + 1], ALU.mult, ALU.add)
            v.tensor_scalar(turns[:, 1, :], angle[:, 1, :], 1 / TURN, None, ALU.mult)
            c.link(dve, v.tensor_scalar(turns[:, 2, :], angle[:, 2, :], 1 / TURN, 0.25, ALU.mult, ALU.add))
            c.link(dve, v.tensor_scalar(turns[:, :, :], turns[:, :, :], MAGIC, None, ALU.add))
            c.link(dve, v.tensor_scalar(turns[:, :, :], turns[:, :, :], MAGIC, None, ALU.subtract))
            for part in (TURN1, TURN2, TURN3):
                c.link(dve, v.scalar_tensor_tensor(out=angle[:, :, :], in0=turns[:, :, :], scalar=-part,
                                                   in1=angle[:, :, :], op0=ALU.mult, op1=ALU.add))
            v.tensor_scalar(angle[:, 0, :], angle[:, 0, :], cst[:, C_O0:C_O0 + 1], None, ALU.add)
            c.link(dve, v.tensor_scalar(angle[:, 2, :], angle[:, 2, :], TURN / 4, None, ALU.add))
            v.tensor_scalar(angle[:, :, :], angle[:, :, :], ARC, -ARC, ALU.min, ALU.max).then_inc(angle_ready, 1)

            def silu(t, x):
                c.link(dve, v.scalar_tensor_tensor(out=x, in0=t, scalar=1.0, in1=x, op0=ALU.add, op1=ALU.mult))
                return v.tensor_scalar(x, x, 0.5, None, ALU.mult)

            def plus_col(o, x, name, n):
                return v.tensor_tensor(o, x, col(name, 0, n).unsqueeze(2).to_broadcast([P, n, B]), ALU.add)

            def small(bank, at, n):
                return bank[:, at * B:(at + n) * B].rearrange("p (m b) -> p m b", b=B)

            dve.wait_ge(w1_done, 1)
            plus_col(h1[:, :, :], small(M0, 0, NH), "b1", NH).then_inc(h1_ready, 1)
            dve.wait_ge(embt_ready, 1)
            c.link(dve, v.scalar_tensor_tensor(out=embh[:, :, :], in0=embh[:, :, :], scalar=1.0,
                                               in1=emb[:, :, :], op0=ALU.add, op1=ALU.mult))
            v.tensor_scalar(embh[:, :, :], embh[:, :, :], 0.5, None, ALU.mult).then_inc(embs_ready, 1)
            dve.wait_ge(h1t_ready, 1)
            silu(h1t[:, :, :], h1[:, :, :]).then_inc(h1s_ready, 1)
            dve.wait_ge(xall_loaded, 16)
            for i in range(B // 2):
                v.bn_stats(bns[:, i, :], xall[:, i, :])
            dve.wait_ge(w2_done, 1)
            v.tensor_copy(row, M1[0:B, :]).then_inc(row_ready, 1)
            dve.wait_ge(w2t_done, 1)
            plus_col(h2[:, :, :], small(M1, 0, NH), "b2", NH).then_inc(h2_ready, 1)
            for i in range(B // 2, B):
                last = v.bn_stats(bns[:, i, :], xall[:, i, :])
            c.link(dve, last)
            for i in range(B):
                last = v.bn_aggr(bna[:, i, :], bns[:, i, :])
            c.link(dve, last)
            v.tensor_copy(st1[:, 0, :], bna[:, :, 0])
            c.link(dve, v.tensor_tensor(st1[:, 1, :], bna[:, :, 0], bna[:, :, 0], ALU.mult))
            v.tensor_tensor(st1[:, 1, :], st1[:, 1, :], bna[:, :, 1], ALU.add).then_inc(st1_ready, 1)
            dve.wait_ge(wsc_done, 1)
            v.tensor_copy(row, M0[0:B, :]).then_inc(row_ready, 1)
            dve.wait_ge(wsct_done, 1)
            plus_col(half_sc[:, :, :], small(M0, 0, NC), "bsc", NC)
            c.link(dve, plus_col(half_sh[:, :, :], small(M0, NC, NC), "bsh", NC))
            v.tensor_scalar(half_sc[:, :, :], half_sc[:, :, :], 0.5, None, ALU.mult)
            c.link(dve, v.tensor_scalar(half_sh[:, :, :], half_sh[:, :, :], 0.5, None, ALU.mult))
            dve.wait_ge(st1_done, 1)
            c.link(dve, v.tensor_copy(mean1[:, :], M2[:, 0:B]))
            c.link(dve, v.tensor_tensor(var1[:, :], mean1[:, :], mean1[:, :], ALU.mult))
            c.link(dve, v.scalar_tensor_tensor(out=var1[:, :], in0=var1[:, :], scalar=-1.0, in1=M2[:, B:2 * B],
                                               op0=ALU.mult, op1=ALU.add))
            v.tensor_scalar(var1[:, :], var1[:, :], EPS, None, ALU.add).then_inc(var1_ready, 1)
            dve.wait_ge(std1_ready, 1)
            c.link(dve, v.reciprocal(rstd1[:, :], rstd1[:, :]))
            dve.wait_ge(layer0_loaded, 32)

            def late_setup():
                c = v_late.start(0)
                dve.wait_ge(wada_done, 1)
                c.link(dve, plus_col(ada[:, :, :], small(M1, 0, 2 * NC), "ada", 2 * NC))
                v.tensor_scalar(ada[:, 0:NC, :], ada[:, 0:NC, :], 1.0, None, ALU.add)
                v.tensor_scalar(bq4[:, :], col("bq", 0, NC), DH ** -0.5, None, ALU.mult)\
                 .then_inc(setup_ready, 1)
                dve.wait_ge(bov_done, 1)
                v.tensor_tensor(bov[:, :], M1[:, 0:NC], col("bo", 0, NC), ALU.add).then_inc(bov_ready, 1)

            def softmax_max(b, n):
                h = head_at(n)[0]
                dve.wait_ge(qk_done, 16 * b + n + 1)
                dve.wait_ge(bias_ready, 16 * b + n + 1)
                need(dve, exp_done, 16 * b + n - 1)
                for t in range(NC):
                    if t == 0:
                        hold(dve)
                    last = v.tensor_tensor_reduce(
                        out=sneg[:, n % 2, t, :], in0=score[n % 2][:, t * S:(t + 1) * S],
                        in1=bias[:, n // GH, n % GH, t * S:(t + 1) * S], scale=-1.0, scalar=HUGE,
                        op0=ALU.add, op1=ALU.min, accum_out=negmax[:, t, h:h + 1])
                last.then_inc(smax_done, 1)

            def probs_out(b, n):
                dve.wait_ge(tr_done, 16 * b + n + 1)
                need(dve, pv_done, 4 * b + n // GH - 1)
                v.tensor_copy(probT[:, n % 8, :], trans[n % 2][:, :]).then_inc(pt_dve, 1)

            def apply(b, k, src, mean, rstd):
                c = v_apply.start(b, 2 * k)
                need(dve, hin_ready, 2 * b + k)
                c.link(dve, v.scalar_tensor_tensor(out=lna[:, :], in0=src, scalar=mean, in1=gb[:, 0, :],
                                                   op0=ALU.subtract, op1=ALU.mult))
                c.link(dve, v.scalar_tensor_tensor(out=lna[:, :], in0=lna[:, :], scalar=rstd, in1=gb[:, 1, :],
                                                   op0=ALU.mult, op1=ALU.add))
                for m in range(NC):
                    last = v.tensor_scalar(lny[:, m * S:(m + 1) * S], lna[:, m * S:(m + 1) * S],
                                           half_sc[:, m, bass.ds(b, 1)], half_sh[:, m, bass.ds(b, 1)],
                                           ALU.mult, ALU.add)
                last.then_inc(y_ready, 1)

            def silu_out(b, k):
                dve.wait_ge(tanh_ready, 2 * b + 1 + k)
                if k == 0:
                    need(dve, wout_done, b)
                else:
                    dve.wait_ge(win_done, b + 1)
                v.scalar_tensor_tensor(out=hin[:, :], in0=lnt[:, :], scalar=1.0, in1=lny[:, :],
                                       op0=ALU.add, op1=ALU.mult).then_inc(hin_ready, 1)

            def seed(b, c, t, seeded):
                c.link(dve, v.tensor_scalar(t["h"][:, :], t["v"][:, :].bitcast(I32), 1, None,
                                            ALU.arith_shift_right))
                v.tensor_scalar(t["s"][:, :], t["h"][:, :], -1.0, SEED, ALU.mult, ALU.add).then_inc(seeded, 1)

            def token_stats(b, chain, t, x, seeded):
                c = chain.start(b)
                for i in range(NC):
                    last = v.bn_stats(t["bs"][:, i, :], x[:, i, :])
                c.link(dve, last)
                hold(dve)
                for i in range(NC):
                    last = v.bn_aggr(t["ba"][:, i, :], t["bs"][:, i, :])
                c.link(dve, last)
                c.link(dve, v.tensor_scalar(t["v"][:, :], t["ba"][:, :, 1], EPS, None, ALU.add))
                seed(b, c, t, seeded)

            def newton_here(b, call, t, n, seeded, done):
                dve.wait_ge(seeded, b + 1)
                newton(dve, v, v_newton.start(call), t, n, done)

            def token_norm(o, x, t):
                for i in range(NC):
                    last = v.tensor_scalar(o[:, i * D:(i + 1) * D], x[:, i, :], t["ba"][:, i, 0:1],
                                           t["r"][:, i:i + 1], ALU.subtract, ALU.mult)
                return last

            def output(b):
                dve.wait_ge(ff2_done, b)
                dve.wait_ge(x2b_ready, b)
                v.tensor_tensor(outt[:, :], M1[:, :], x2b[:, :], ALU.add).then_inc(out_ready, 1)

            def before(b, s, att, proj, layer0, post, finish):
                n1, n2 = b + 1, b + 2
                if s == 2 and proj and not att:
                    late_setup()
                if s == 0 and post:
                    dve.wait_ge(exp_done, 16 * b)
                    v.reciprocal(rinv[:, :, :], rsum[:, :, :]).then_inc(rinv_ready, 1)
                    dve.wait_ge(rinv_ready, b)
                    need(dve, r_done, b - 1)
                    v.tensor_copy(rinvx[:, :, :, :], rinv[:, :, :].unsqueeze(3).to_broadcast([P, NC, H, DH]))\
                     .then_inc(rinvx_ready, 1)
                if s == 11 and layer0:
                    silu_out(n2, 0)
                if s in (9, 10) and proj:
                    i = s - 9
                    dve.wait_ge(hi_ready, 2 * n1 + 1 + i)
                    need(dve, parts_stored, 32 * n1)
                    for c in range(NC):
                        at = slice(c * S, (c + 1) * S)
                        last = v.scalar_tensor_tensor(out=qk_part[:, i, LO, at], in0=(M2, M0)[i][:, at],
                                                      scalar=bq4[:, c:c + 1] if i == 0 else col("bk", c),
                                                      in1=qk_part[:, i, HI, at].bitcast(F32),
                                                      op0=ALU.add, op1=ALU.subtract)
                    last.then_inc(lo_ready, 1)
                if s == 1 and finish:
                    output(b - 1)
                if s == 9 and finish:
                    dve.wait_ge(out_stored, 16 * (b - 1))
                    hold(dve)
                if s == 0 and proj:
                    silu_out(n1, 1)
                if s == 12 and layer0:
                    c = v_ln2a.start(n2)
                    dve.wait_ge(mid_ready, 2 * n2 + 2)
                    c.link(dve, v.bn_stats(mst[:, :], mid[:, :]))
                    hold(dve)
                    c.link(dve, v.bn_aggr(ln2["ba"][:, 0, :], mst[:, :]))
                    v.tensor_copy(mag[:, 0:1], ln2["ba"][:, 0, 0:1])
                    v.scalar_tensor_tensor(out=mag[:, 1:2], in0=ln2["ba"][:, 0, 0:1], scalar=ln2["ba"][:, 0, 0:1],
                                           in1=ln2["ba"][:, 0, 1:2], op0=ALU.mult, op1=ALU.add)\
                     .then_inc(mst_ready, 1)

            def after(b, s, att, proj, layer0, post, finish):
                n1, n2 = b + 1, b + 2
                if s == 14 and layer0:
                    dve.wait_ge(rs2, n2 + 1)
                    apply(n2, 1, mid[:, :], mst2[:, 0:1], ln2["r"][:, 0:1])
                if s == 3 and proj:
                    dve.wait_ge(wout_done, n1 + 1)
                    dve.wait_ge(xb_ready, n1 + 1)
                    v.tensor_tensor(x1[:, :, :], halves(M0), halves(xb), ALU.add).then_inc(x1_ready, 1)
                    dve.wait_ge(x1_ready, n1 + 1)
                    token_stats(n1, v_ln3, ln3, x1, seed3)
                    if not att:
                        newton_here(n1, 1, ln3, NC, seed3, rs3)
                if s == 7 and post:
                    dve.wait_ge(rs4, b)
                    token_norm(x2n, x2, ln4).then_inc(x2n_ready, 1)
                if s == 5 and post:
                    dve.wait_ge(x2_ready, b)
                    token_stats(b - 1, v_ln4, ln4, x2, seed4)
                    if not att:
                        newton_here(b - 1, 3, ln4, NC, seed4, rs4)
                if s == 3 and post:
                    dve.wait_ge(pv_done, 4 * b)
                    dve.wait_ge(r_ready, b)
                    v.tensor_tensor(ctxT[:, :, :], halves(context), halves(rbc), ALU.mult).then_inc(ctx_ready, 1)
                if s == 8 and layer0:
                    dve.wait_ge(x_loaded, 32 * n2 + 32)
                    apply(n2, 0, xf[:, :], mean1[:, bass.ds(n2, 1)], rstd1[:, bass.ds(n2, 1)])
                if s == 12 and layer0:
                    c = v_ln2b.start(n2)
                    dve.wait_ge(mst_done, n2 + 1)
                    c.link(dve, v.tensor_copy(mst2[:, :], M0[:, 0:2]))
                    c.link(dve, v.scalar_tensor_tensor(out=ln2["a"][:, :], in0=mst2[:, 0:1], scalar=mst2[:, 0:1],
                                                       in1=mst2[:, 1:2], op0=ALU.mult, op1=ALU.subtract))
                    c.link(dve, v.tensor_scalar(ln2["v"][:, :], ln2["a"][:, :], -1.0, EPS, ALU.mult, ALU.add))
                    seed(n2, c, ln2, seed2)
                    if not att:
                        newton_here(n2, 2 * (n2 == 1), ln2, 1, seed2, rs2)
                if s in (10, 11, 12, 13) and post:
                    j = s - 10
                    dve.wait_ge(uth_ready, 4 * b - 4 + j + 1)
                    if j == 0:
                        need(dve, ff2_done, b - 1)
                    v.scalar_tensor_tensor(out=fT[:, 2 * j:2 * j + 2, :], in0=uth[:, 2 * j:2 * j + 2, :],
                                           scalar=1.0, in1=uT[:, 2 * j:2 * j + 2, :], op0=ALU.add,
                                           op1=ALU.mult).then_inc(f_ready, 1)
                if s == 6 and proj:
                    dve.wait_ge(rs3, n1 + 1)
                    need(dve, nt_done, n1)
                    token_norm(xn, x1, ln3).then_inc(xn_ready, 1)
                if s == 15 and post and not att:
                    output(b)

            def turn(b, att, proj, layer0, post, finish):
                for s in range(16):
                    if att:
                        softmax_max(b, s)
                    before(b, s, att, proj, layer0, post, finish)
                    if (att if s >= LAG else post) and (s - LAG) % 16 not in ACT_MOVES:
                        probs_out(b - (s < LAG), (s - LAG) % 16)
                    after(b, s, att, proj, layer0, post, finish)

            turns_of_the_loop(dve, turn)


def kernel(**inputs):
    import numpy as np
    import concourse.bacc as bacc
    from concourse.bass_utils import run_bass_kernel_spmd as run

    a = {k: np.asarray(x) for k, x in inputs.items()}

    def columns(x):
        return x.reshape(-1, P).T

    def rows_of(x):
        return x.reshape(-1, P, x.shape[1]).transpose(1, 0, 2).reshape(P, -1)

    half0, half1 = E // 2, D // 2
    f0 = np.exp(np.arange(half0, dtype=np.float32) * np.float32(-np.log(10000.0) / (half0 - 1)))
    f1 = np.exp(np.arange(half1, dtype=np.float32) * np.float32(-np.log(10000.0) / (half1 - 1)))
    consts = np.zeros((P, NCST), np.float32)
    consts[:, C_F0] = np.concatenate([f0, f0])
    consts[half0:, C_T0] = 0.25
    consts[half0:, C_O0] = TURN / 4
    consts[:, C_F1] = f1

    x = a["x"]
    order = [head_at(n)[0] for n in range(H)]
    fside = a["fside_Bx16xSxS_0"][:, order].reshape(B, GROUPS, GH, NC, P, S).transpose(0, 1, 4, 2, 3, 5)
    l0, l1 = "L0_cond_", "L1_cond_"
    arrays = {
        "x_tok": x.reshape(B, NC, P, D).transpose(0, 2, 1, 3).reshape(B, P, NC * D),
        "x_feat": x.transpose(0, 2, 1).reshape(B, NC, P, S).transpose(0, 2, 1, 3).reshape(B, P, NC * S),
        "cond_t": a["condB_t"],
        "step_t": a["itok_B_34_63"],
        "fside": fside.reshape(B, GROUPS, P, GH, NC * S),
        "mask": a["mask_Bx1xSxS_bk0"].reshape(B, NC, P, S).transpose(0, 2, 1, 3).reshape(B, P, NC * S),
        "gbT": np.stack([rows_of(a[l0 + n].T) for n in ("gamma", "beta")], 1),
        "wmain": np.concatenate([rows_of(a[n]) for n in (
            l0 + "W_in", l0 + "W_out", l1 + "Wq", l1 + "Wk", l1 + "Wv", l1 + "Wo", l1 + "W1", l1 + "W2")], 1),
        "wcond": np.concatenate([rows_of(a[n]) for n in (
            l0 + "W1", l0 + "W2", l0 + "Wsc", l0 + "Wsh", l1 + "W_ada")], 1),
        "vecs": np.concatenate([columns(a[n]) for n in (
            l0 + "b1", l0 + "b2", l0 + "bsc", l0 + "bsh", l0 + "b_in", l1 + "b_ada", l1 + "bq", l1 + "bk",
            l1 + "bv", l1 + "bo", l1 + "b1", l1 + "g2", l1 + "beta2")], 1),
        "consts": consts,
        "rows": np.stack([a[l0 + "b_out"], a[l1 + "b2"]]),
    }
    nc = bacc.Bacc("TRN2", target_bir_lowering=False, num_devices=1)
    args, fed = [], {}
    for name, value in arrays.items():
        value = np.ascontiguousarray(value)
        fed[f"in_{name}"] = value
        args.append(nc.dram_tensor(f"in_{name}", value.shape, mybir.dt.from_np(value.dtype),
                                   kind="ExternalInput").ap())
    out = nc.dram_tensor("out", (B, P, NC * D), F32, kind="ExternalOutput").ap()
    build(nc, *args, out)
    got = run(nc, [fed], core_ids=[0]).results[0]["out"]
    return np.ascontiguousarray(got.reshape(B, P, NC, D).transpose(0, 2, 1, 3).reshape(B, S, D))
```
